# Optimizing a Trainium2 kernel written in Bass

```python
import numpy as np
import jax
import jax.numpy as jnp

def _softmax(x, axis=-1):
    return jax.nn.softmax(x, axis=axis)

def _gelu(x):
    return jax.nn.gelu(x, approximate=True)

def _silu(x):
    return jax.nn.silu(x)

def _sigmoid(x):
    return jax.nn.sigmoid(x)

def _layernorm(x, axis=-1, eps=1e-05):
    m = jnp.mean(x, axis=axis, keepdims=True)
    v = jnp.var(x, axis=axis, keepdims=True)
    return (x - m) / jnp.sqrt(v + eps)

def _scatter_add(tgt, idx, src, axis=0):
    return tgt.at[idx].add(src)

def _segment_sum(src, seg, n):
    return jax.ops.segment_sum(src, seg, n)
kernel_name = 'mk_cond_resid_d2_seqx_r4_dbf965'

def setup_inputs(seed: int=0):
    np.random.seed(seed)
    _w = jnp.asarray

    def _rec_inputs():
        import jax
        import jax.numpy as jnp
        _rk = jax.random.key(seed)
        x = 7.22e-05 + 1 * jax.random.normal(jax.random.fold_in(_rk, 1), (8, 512, 256), jnp.float32)
        _lenS = 512 - jax.random.randint(jax.random.fold_in(_rk, 7), (8,), 0, max(1, 512 // 4) + 1, jnp.int32)
        _lenS2 = 512 - jax.random.randint(jax.random.fold_in(_rk, 8), (8,), 0, max(1, 512 // 4) + 1, jnp.int32)
        condB_tauraws = -5.74692 + 0.777674 * jax.random.normal(jax.random.fold_in(_rk, 11), (8,), jnp.float32)
        cond_256 = -0.000235209 + 0.019331 * jax.random.normal(jax.random.fold_in(_rk, 12), (8, 64), jnp.float32)
        condB_bn2 = jnp.zeros((8,), jnp.float32)
        cond_1024 = -4.10585e-05 + 0.0199478 * jax.random.normal(jax.random.fold_in(_rk, 14), (8, 256), jnp.float32)
        itok_B_0_2 = jax.random.randint(jax.random.fold_in(_rk, 15), (8,), 0, 3, jnp.int32)
        return (x, condB_tauraws, cond_256, condB_bn2, cond_1024, itok_B_0_2)
    x, condB_tauraws, cond_256, condB_bn2, cond_1024, itok_B_0_2 = _rec_inputs()

    def _L0_cond_setup():
        import jax, jax.numpy as jnp
        import numpy as np
        import math
        B, T, E, D = (4, 512, 256, 4)

        def _tau_init(t):
            a = 0.1 ** (1.0 / max(t - 1, 1))
            tt = -math.log(max(a, 1e-10))
            return math.log(math.exp(tt) - 1 + 1e-10)

        def causal_ema(b, tau_raw):
            alpha = jnp.exp(-jax.nn.softplus(tau_raw)).astype(b.dtype)

            def step(h, bt):
                h = alpha * h + bt
                return (h, h)
            h0 = jnp.zeros((b.shape[0], b.shape[2]), b.dtype)
            _, hs = jax.lax.scan(step, h0, jnp.swapaxes(b, 0, 1))
            return jnp.swapaxes(hs, 0, 1)
        key = jax.random.key(seed)
        ks = jax.random.split(key, 10)
        s = 0.02
        return {'x': jax.random.normal(ks[0], (B, T, E), jnp.float32), 'tau_ctx': jnp.float32(_tau_init(max(T // 2, 4))), 'tau_raws': jnp.array([_tau_init(max(T // 2 ** i, 2)) for i in range(D)], jnp.float32), 'Wg': jax.random.normal(ks[1], (E, 2 * E), jnp.float32) * s, 'bg': jnp.full((E,), -0.5, jnp.float32), 'Wn1': jax.random.normal(ks[2], (E // 4, E), jnp.float32) * s, 'bn1': jnp.zeros((E // 4,), jnp.float32), 'Wn2': jax.random.normal(ks[3], (D, E // 4), jnp.float32) * s, 'bn2': jnp.zeros((D,), jnp.float32), 'blend': jax.random.normal(ks[4], (D, E), jnp.float32) * s, 'Wsoma': jax.random.normal(ks[5], (E, E), jnp.float32) * s, 'bsoma': jnp.zeros((E,), jnp.float32), 'Wtemp': jax.random.normal(ks[6], (E, E), jnp.float32) * s, 'btemp': jnp.zeros((E,), jnp.float32), 'Wout': jax.random.normal(ks[7], (E, E), jnp.float32) * s, 'gamma': jnp.ones((E,), jnp.float32), 'beta': jnp.zeros((E,), jnp.float32)}
    _L0_cond_all = _L0_cond_setup()
    _L0_cond_in = {k: v for k, v in _L0_cond_all.items() if k in ('tau_ctx', 'Wg', 'bg', 'Wn1', 'bn1', 'Wsoma', 'bsoma', 'Wtemp', 'btemp', 'Wout', 'gamma', 'beta')}
    del _L0_cond_all

    def _L1_cond_setup():
        import jax, jax.numpy as jnp
        import numpy as np
        B, S, D, F, E = (8, 256, 256, 1024, 4)

        def _dense(x, wi, wo):
            return jax.nn.relu(x @ wi) @ wo
        key = jax.random.key(seed)
        ks = jax.random.split(key, 10)
        scale = 0.02
        return {'hidden_states': jax.random.normal(ks[0], (B, S, D), jnp.float32), 'type_idx': jax.random.randint(ks[1], (B,), 0, 3, jnp.int32), 'expert_wi': jax.random.normal(ks[2], (E, D, F), jnp.float32) * scale, 'expert_wo': jax.random.normal(ks[3], (E, F, D), jnp.float32) * scale, 'share_wi': jax.random.normal(ks[4], (3, D, F), jnp.float32) * scale, 'share_wo': jax.random.normal(ks[5], (3, F, D), jnp.float32) * scale, 'gate_vecs': jnp.array([[0.22, 0.22, 0.2, 0.2], [0.2, 0.22, 0.22, 0.2], [0.2, 0.2, 0.22, 0.22]], jnp.float32), 'gate_w1': jax.random.normal(ks[6], (4 * D, D), jnp.float32) * scale, 'gate_w2': jax.random.normal(ks[7], (D, 4), jnp.float32) * scale}
    _L1_cond_all = _L1_cond_setup()
    _L1_cond_in = {k: v for k, v in _L1_cond_all.items() if k in ('expert_wi', 'expert_wo', 'share_wi', 'share_wo', 'gate_vecs', 'gate_w1', 'gate_w2')}
    del _L1_cond_all
    return {'x': x, 'condB_tauraws': condB_tauraws, 'cond_256': cond_256, 'condB_bn2': condB_bn2, 'cond_1024': cond_1024, 'itok_B_0_2': itok_B_0_2, 'L0_cond_tau_ctx': _L0_cond_in['tau_ctx'], 'L0_cond_Wg': _L0_cond_in['Wg'], 'L0_cond_bg': _L0_cond_in['bg'], 'L0_cond_Wn1': _L0_cond_in['Wn1'], 'L0_cond_bn1': _L0_cond_in['bn1'], 'L0_cond_Wsoma': _L0_cond_in['Wsoma'], 'L0_cond_bsoma': _L0_cond_in['bsoma'], 'L0_cond_Wtemp': _L0_cond_in['Wtemp'], 'L0_cond_btemp': _L0_cond_in['btemp'], 'L0_cond_Wout': _L0_cond_in['Wout'], 'L0_cond_gamma': _L0_cond_in['gamma'], 'L0_cond_beta': _L0_cond_in['beta'], 'L1_cond_expert_wi': _L1_cond_in['expert_wi'], 'L1_cond_expert_wo': _L1_cond_in['expert_wo'], 'L1_cond_share_wi': _L1_cond_in['share_wi'], 'L1_cond_share_wo': _L1_cond_in['share_wo'], 'L1_cond_gate_vecs': _L1_cond_in['gate_vecs'], 'L1_cond_gate_w1': _L1_cond_in['gate_w1'], 'L1_cond_gate_w2': _L1_cond_in['gate_w2']}

def reference(x, condB_tauraws, cond_256, condB_bn2, cond_1024, itok_B_0_2, L0_cond_tau_ctx, L0_cond_Wg, L0_cond_bg, L0_cond_Wn1, L0_cond_bn1, L0_cond_Wsoma, L0_cond_bsoma, L0_cond_Wtemp, L0_cond_btemp, L0_cond_Wout, L0_cond_gamma, L0_cond_beta, L1_cond_expert_wi, L1_cond_expert_wo, L1_cond_share_wi, L1_cond_share_wo, L1_cond_gate_vecs, L1_cond_gate_w1, L1_cond_gate_w2):
    import jax
    import jax.numpy as jnp

    def _L0_cond_ref(x, tau_ctx, tau_raws, Wg, bg, Wn1, bn1, Wn2, bn2, blend, Wsoma, bsoma, Wtemp, btemp, Wout, gamma, beta):
        import jax, jax.numpy as jnp
        import numpy as np
        import math
        B, T, E, D = (4, 512, 256, 4)

        def _tau_init(t):
            a = 0.1 ** (1.0 / max(t - 1, 1))
            tt = -math.log(max(a, 1e-10))
            return math.log(math.exp(tt) - 1 + 1e-10)

        def causal_ema(b, tau_raw):
            alpha = jnp.exp(-jax.nn.softplus(tau_raw)).astype(b.dtype)

            def step(h, bt):
                h = alpha * h + bt
                return (h, h)
            h0 = jnp.zeros((b.shape[0], b.shape[2]), b.dtype)
            _, hs = jax.lax.scan(step, h0, jnp.swapaxes(b, 0, 1))
            return jnp.swapaxes(hs, 0, 1)
        ctx = causal_ema(x, tau_ctx)
        gate_in = jnp.concatenate([x, ctx], axis=-1)
        wg = jax.nn.sigmoid(jnp.einsum('btc,ec->bte', gate_in, Wg) + bg)
        gated = x * wg
        h1 = jax.nn.gelu(jnp.einsum('btc,hc->bth', x, Wn1) + bn1, approximate=False)
        mod = 0.5 + jax.nn.sigmoid(jnp.einsum('bth,dh->btd', h1, Wn2) + bn2)
        traces = jax.vmap(lambda tau, m: causal_ema(gated * m[..., None], tau))(tau_raws, jnp.moveaxis(mod, -1, 0))
        blend_w = jax.nn.softmax(blend, axis=0)
        temporal = jnp.einsum('dbtc,dc->btc', traces, blend_w)
        gate = jax.nn.sigmoid(jnp.einsum('btc,ec->bte', temporal, Wtemp) + btemp)
        soma = jax.nn.gelu(jnp.einsum('btc,ec->bte', x, Wsoma) + bsoma, approximate=False)
        out = jnp.einsum('btc,ec->bte', soma * gate, Wout)
        mu = out.mean(-1, keepdims=True)
        var = out.var(-1, keepdims=True)
        return (out - mu) / jnp.sqrt(var + 1e-05) * gamma + beta

    def _L1_cond_ref(hidden_states, type_idx, expert_wi, expert_wo, share_wi, share_wo, gate_vecs, gate_w1, gate_w2):
        import jax, jax.numpy as jnp
        import numpy as np
        B, S, D, F, E = (8, 256, 256, 1024, 4)

        def _dense(x, wi, wo):
            return jax.nn.relu(x @ wi) @ wo
        s0 = _dense(hidden_states, share_wi[0], share_wo[0])
        s1 = _dense(hidden_states, share_wi[1], share_wo[1])
        s2 = _dense(hidden_states, share_wi[2], share_wo[2])
        idx_a = type_idx
        idx_b = type_idx + 1
        out_a = jnp.einsum('bsf,bfd->bsd', jax.nn.relu(jnp.einsum('bsd,bdf->bsf', hidden_states, expert_wi[idx_a])), expert_wo[idx_a])
        out_b = jnp.einsum('bsf,bfd->bsd', jax.nn.relu(jnp.einsum('bsd,bdf->bsf', hidden_states, expert_wi[idx_b])), expert_wo[idx_b])
        p = jax.nn.softmax(gate_vecs / 0.1, axis=-1)
        wa = p[type_idx, idx_a][:, None, None]
        wb = p[type_idx, idx_b][:, None, None]
        expert_out = out_a * wa + out_b * wb
        gi = jnp.concatenate([expert_out[:, 0], s0[:, 0], s1[:, 0], s2[:, 0]], axis=-1)
        g = jax.nn.softmax(jax.nn.relu(gi @ gate_w1) @ gate_w2, axis=-1)
        out = expert_out * g[:, 0, None, None] + s0 * g[:, 1, None, None] + s1 * g[:, 2, None, None] + s2 * g[:, 3, None, None]
        return out
    x = x + _L0_cond_ref(x, L0_cond_tau_ctx, condB_tauraws, L0_cond_Wg, L0_cond_bg, L0_cond_Wn1, L0_cond_bn1, cond_256, condB_bn2, cond_1024, L0_cond_Wsoma, L0_cond_bsoma, L0_cond_Wtemp, L0_cond_btemp, L0_cond_Wout, L0_cond_gamma, L0_cond_beta)
    x = x + _L1_cond_ref(x, itok_B_0_2, L1_cond_expert_wi, L1_cond_expert_wo, L1_cond_share_wi, L1_cond_share_wo, L1_cond_gate_vecs, L1_cond_gate_w1, L1_cond_gate_w2)
    return x

_drawn_inputs = setup_inputs


def setup_inputs(seed=0):
    import zlib

    import numpy as np

    out = dict(_drawn_inputs(seed))
    spreads = {'condB_bn2': (0.0, 2.0),
     'L0_cond_bg': (-0.5, 0.6),
     'L0_cond_bn1': (0.0, 2.0),
     'L0_cond_bsoma': (0.0, 0.1),
     'L0_cond_btemp': (0.0, 0.336),
     'L0_cond_gamma': (1.0, 0.2),
     'L0_cond_beta': (0.0, 0.1)}
    factors = {'condB_tauraws': 8.0,
     'cond_256': 8.0,
     'cond_1024': 44.502,
     'L0_cond_Wn1': 8.0,
     'L1_cond_expert_wi': 4.935,
     'L1_cond_expert_wo': 4.151,
     'L1_cond_gate_vecs': 40.102,
     'L1_cond_gate_w1': 8.0,
     'L1_cond_gate_w2': 8.0}
    for name, (base, spread) in spreads.items():
        noise = np.random.default_rng([zlib.crc32(name.encode()), seed]).standard_normal(out[name].shape)
        drawn = base * np.exp(spread * noise) if base else spread * noise
        out[name] = jnp.asarray(drawn.astype(out[name].dtype))
    for name, factor in factors.items():
        out[name] = (out[name] * factor).astype(out[name].dtype)
    return out
```

```python
from contextlib import ExitStack

import numpy as np

import concourse.bass as bass
from concourse import mybir

ALU = mybir.AluOpType
ACT = mybir.ActivationFunctionType
F32 = mybir.dt.float32
F32R = mybir.dt.float32r
I32 = mybir.dt.int32
AX_X = mybir.AxisListType.X

P = 128
B, T, E = 8, 512, 256
CT = E // P
D = 8
H1 = 64
F = 1024
NE = 4
NS = 3
TYPES = 3
FFNS = NS + 2
UF = F // 2
UT = UF // P
UNITS = FFNS * F // UF
TPF = F // P
SLOTS = FFNS * TPF
LAG = 2
NU = 4
TT = T // P
LN_EPS = 1e-5

W_GATE, W_SOMA, W_TEMP, W_OUT, W_N1, W_N2, W_ALL = np.cumsum(
    [0, 2 * CT * E, CT * E, CT * E, CT * E, CT * P, P]).tolist()
(C_BG, C_BSOMA, C_BTEMP, C_GAMMA, C_BETA, C_BN1, C_BN2, C_BLEND, C_TAU, C_GV, C_GW2, C_ALL) = np.cumsum(
    [0, CT, CT, CT, CT, CT, 1, 1, CT * D, D + 1, TYPES * NE, CT * 4]).tolist()

PLAN_TENSOR = {
    2: ["soma"], 3: ["gate_hidden"], 4: ["gate_logits"], 5: ["mod_hidden"], 7: ["mod"], 8: ["wgate"],
    28: ["tgate"], 31: ["out"], 34: ["turn"],
}
PLAN_SCALAR = {
    1: ["x_hi"], 3: ["soma", "ctx_hi"], 5: ["gate_exp"], 6: ["mod_hidden"], 8: ["mod"], 9: ["wgate"],
    27: ["temp_hi"], 29: ["tgate"], 30: ["sg_hi"], 33: ["ln_sqrt"], 35: ["turn"], 36: ["x2_hi"],
}
PLAN_VECTOR = {
    1: ["gate_part", "x_lo"], 2: ["ctx_scan"], 3: ["gate_spread", "ctx_lo"], 4: ["gate_max"],
    5: ["gate_soft", "mix01"], 6: ["mod_hidden_lo", "mix2"], 7: ["mix3"], 10: ["gated"],
    27: ["temp_lo"], 30: ["sg", "sg_lo"], 32: ["ln_stats"], 33: ["ln_norm"], 36: ["x2", "x2_lo"],
}
for _d in range(D):
    PLAN_VECTOR[11 + 2 * _d] = [f"ema_in{_d}"]
    PLAN_VECTOR[12 + 2 * _d] = [f"ema_out{_d}"]
PLAN_SYNC = {
    0: ["x"], 7: ["store"], 8: ["mod"], 9: ["modb0", "modb1"], 14: ["modb2"], 18: ["modb3"],
}
LAST_SLOT = 36
GATING = {"gate_hidden", "gate_logits", "gate_exp", "gate_part", "gate_spread", "gate_max", "gate_soft",
          "mix01", "mix2", "mix3", "store"}


def later(count):
    return not isinstance(count, int) or count > 0


class Period:

    def __init__(self, n, f, n_parity, f_parity, aux_before):
        self.n, self.f, self.n_parity, self.f_parity = n, f, n_parity, f_parity
        order = []
        if n is not None:
            order += ["soma"]
        if f is not None:
            order += ["gating"]
        if n is not None:
            order += ["mod", "wgate", "tgate", "out", "turn"]
        self.aux = {name: aux_before + i for i, name in enumerate(order)}

    def steps(self, plan, slot):
        for name in plan.get(slot, ()):
            if (self.f if name in GATING else self.n) is not None:
                yield name


def build(nc, x, w_ctx, params, types_row, types_all, shared_wi, shared_wo, expert_wi, expert_wo,
          gate_w1, out):
    mod_scratch = nc.dram_tensor("mod_scratch", [D, T], F32, kind="Internal").ap()

    with ExitStack() as ctx:
        def sb(name, shape, dt=F32):
            return ctx.enter_context(nc.sbuf_tensor(name, shape, dt))

        def sem(name):
            return ctx.enter_context(nc.semaphore(name))

        def sems(name, n):
            return [sem(f"{name}{i}") for i in range(n)]

        raw_wi = sb("raw_wi", [P, 2, CT * UF])
        raw_wo = sb("raw_wo", [P, 2, UT * E])
        wi_hi = sb("wi_hi", [P, 2, CT * UF], F32R)
        wi_lo = sb("wi_lo", [P, 2, CT * UF], F32R)
        wo_hi = sb("wo_hi", [P, 2, UT * E], F32R)
        wo_lo = sb("wo_lo", [P, 2, UT * E], F32R)
        hid_hi = sb("hid_hi", [P, NU, T], F32R)
        hid_lo = sb("hid_lo", [P, NU, T], F32R)
        wc_hi = sb("wc_hi", [P, W_ALL], F32R)
        wc_lo = sb("wc_lo", [P, W_ALL], F32R)
        gw1 = sb("gw1", [P, 8, E])
        par = sb("par", [P, C_ALL])
        types_sb = sb("types_sb", [1, B], I32)
        types_b = sb("types_b", [P, B], I32)
        types_f = sb("types_f", [P, B])
        y = sb("y", [P, 4, CT, T])
        x2 = sb("x2", [P, 2, CT, T])
        x2_hi = sb("x2_hi", [P, 2, CT, T], F32R)
        x2_lo = sb("x2_lo", [P, 2, CT, T], F32R)
        xt = sb("xt", [P, CT, T])
        xg_hi = sb("xg_hi", [P, CT, T], F32R)
        xg_lo = sb("xg_lo", [P, CT, T], F32R)
        ct_hi = sb("ct_hi", [P, CT, T], F32R)
        ct_lo = sb("ct_lo", [P, CT, T], F32R)
        ctxt = sb("ctxt", [P, CT, T])
        temporal = sb("temporal", [P, CT, T])
        soma = sb("soma", [P, CT, T])
        gates = sb("gates", [P, CT, T])
        trace = sb("trace", [P, CT, T])
        modh = sb("modh", [P, T])
        modh_hi = sb("modh_hi", [P, T], F32R)
        modh_lo = sb("modh_lo", [P, T], F32R)
        mod = sb("mod", [D, T])
        modb = sb("modb", [P, 2, 2, T])
        normed = sb("normed", [P, TT, E])
        ident = sb("ident", [P, P])
        ones = sb("ones", [P, P])
        alpha = sb("alpha", [P, D + 1])
        blend_w = sb("blend_w", [P, CT, D])
        soft = sb("soft", [P, 16])
        pairs = sb("pairs", [P, TYPES, NE])
        pairs_s = sb("pairs_s", [P, 2 * TYPES])
        wab = sb("wab", [P, 2, B])
        picks = sb("picks", [P, TYPES, B])
        wa_now = sb("wa_now", [P, 2])
        gpart = sb("gpart", [P, E])
        gspread = sb("gspread", [P, CT, P])
        gmax = sb("gmax", [P, 1])
        gexp = sb("gexp", [P, 4])
        gsum = sb("gsum", [P, 1])
        grec = sb("grec", [P, 1])
        g = sb("g", [P, 4])
        stats = sb("stats", [P, TT, 6])
        meanvar = sb("meanvar", [P, TT, 2])
        std = sb("std", [P, TT])
        rstd = sb("rstd", [P, TT])
        eps = sb("eps", [P, 1])

        ps_up = [ctx.enter_context(nc.psum_tensor(f"ps_up{i}", [P, T], F32)) for i in range(NU)]
        ps_down = [ctx.enter_context(nc.psum_tensor(f"ps_down{i}", [P, T], F32)) for i in range(CT)]
        ps_aux = [ctx.enter_context(nc.psum_tensor(f"ps_aux{i}", [P, T], F32)) for i in range(2)]

        par_loaded = sem("par_loaded")
        types_loaded = sem("types_loaded")
        wc_loaded = sem("wc_loaded")
        ident_loaded = sem("ident_loaded")
        consts_ready = sem("consts_ready")
        consts_chain = sem("consts_chain")
        alpha_exp = sem("alpha_exp")
        wc_hi_ready = sem("wc_hi_ready")
        wc_ready = sem("wc_ready")
        wi_loaded = sems("wi_loaded", 2)
        wo_loaded = sems("wo_loaded", 2)
        wi_hi_ready = sem("wi_hi_ready")
        wo_hi_ready = sem("wo_hi_ready")
        wi_ready = sem("wi_ready")
        wo_ready = sem("wo_ready")
        up_done = sem("up_done")
        hid_hi_ready = sem("hid_hi_ready")
        hid_ready = sem("hid_ready")
        down_done = sem("down_done")
        y_ready = sem("y_ready")
        experts_ready = sem("experts_ready")
        aux_ready = sems("aux_ready", 2)
        aux_free = sems("aux_free", 2)
        x_loaded = sem("x_loaded")
        x_hi_ready = sem("x_hi_ready")
        x_ready = sem("x_ready")
        ctx_ready = sem("ctx_ready")
        ctx_hi_ready = sem("ctx_hi_ready")
        ctx_split = sem("ctx_split")
        soma_ready = sem("soma_ready")
        modh_ready = sem("modh_ready")
        modh_hi_ready = sem("modh_hi_ready")
        modh_split = sem("modh_split")
        mod_ready = sem("mod_ready")
        mod_stored = sem("mod_stored")
        modb_loaded = sems("modb_loaded", 2)
        wgate_ready = sem("wgate_ready")
        gated_ready = sem("gated_ready")
        ema_in = sem("ema_in")
        ema_trace = sem("ema_trace")
        ema_sum = sem("ema_sum")
        temp_hi_ready = sem("temp_hi_ready")
        temp_split = sem("temp_split")
        tgate_ready = sem("tgate_ready")
        sg_ready = sem("sg_ready")
        sg_hi_ready = sem("sg_hi_ready")
        sg_split = sem("sg_split")
        stats_ready = sem("stats_ready")
        meanvar_ready = sem("meanvar_ready")
        std_ready = sem("std_ready")
        rstd_ready = sem("rstd_ready")
        normed_ready = sem("normed_ready")
        turned_ready = sem("turned_ready")
        x2_ready = sem("x2_ready")
        x2_hi_ready = sem("x2_hi_ready")
        x2_split = sem("x2_split")
        gate_part = sem("gate_part")
        gate_spread = sem("gate_spread")
        gate_max = sem("gate_max")
        gate_exp = sem("gate_exp")
        gate_soft = sem("gate_soft")
        mixed = sem("mixed")
        wa_ready = sem("wa_ready")
        out_stored = sem("out_stored")
        gw1_loaded = sem("gw1_loaded")

        def f32(ap):
            return ap.bitcast(F32)

        def col(c, i=0):
            return par[:, c + i:c + i + 1]

        def drive(eng, mixture, beside):
            aux_ctx, aux_both = 6, 7
            beside_all = lambda p: [beside(s, k, p) for k in range(SLOTS) for s in p_steps(p, k)]

            def p_steps(p, k):
                return list(p.steps(PLANS[eng], k))

            def run(b, parity, p, last):
                for k in range(SLOTS):
                    mixture(b, k, parity, last)
                    for s in p_steps(p, k):
                        beside(s, k, p)

            beside_all(Period(0, None, 0, None, 0))
            yield "mixture starts"
            run(0, 0, Period(1, None, 1, None, aux_ctx), False)
            pairs_of_batches = (B - 2) // 2
            with ENGINES[eng].Fori(0, pairs_of_batches) as i:
                for j in range(2):
                    b = i * 2 + (1 + j)
                    p = Period(i * 2 + (2 + j), i * 2 + j, j % 2, j % 2, i * (2 * aux_both) + (2 * aux_ctx + j * aux_both))
                    run(b, (1 + j) % 2, p, False)
            before = 2 * aux_ctx + (B - 2) * aux_both
            run(B - 1, 1, Period(None, B - 2, None, 0, before), True)
            yield "mixture ends"
            beside_all(Period(None, B - 1, None, 1, before + 1))

        block = ctx.enter_context(nc.Block())
        PLANS = {"sync": PLAN_SYNC, "tensor": PLAN_TENSOR, "scalar": PLAN_SCALAR, "vector": PLAN_VECTOR,
                 "gpsimd": {}}
        ENGINES = {"sync": nc.sync, "tensor": nc.tensor, "scalar": nc.scalar, "vector": nc.vector,
                   "gpsimd": nc.gpsimd}

        def unit_of(b, u):
            if u >= UNITS:
                b, u = b + 1, u - UNITS
            return b, u, b * UNITS + u, u % 2

        @block.sync
        def _(sp):
            expert = {}

            def load_wi(b, u):
                b, u, count, buf = unit_of(b, u)
                if later(count - 1):
                    sp.wait_ge(wi_ready, count - 1)
                sp.dma_start(raw_wi[:, buf, :], source(shared_wi, expert_wi, b, u)).then_inc(wi_loaded[buf], 16)

            def load_wo(b, u):
                b, u, count, buf = unit_of(b, u)
                if later(count - 1):
                    sp.wait_ge(wo_ready, count - 1)
                sp.dma_start(raw_wo[:, buf, :], source(shared_wo, expert_wo, b, u)).then_inc(wo_loaded[buf], 16)

            def source(shared, experts, b, u):
                ffn, half = u // 2, u % 2
                if ffn < NS:
                    return shared[ffn, half]
                if (ffn, half) == (NS, 0) and shared is shared_wi:
                    at = b if isinstance(b, int) else bass.ds(b, 1)
                    cell = types_sb[0:1, b:b + 1] if isinstance(b, int) else types_sb[0:1, at]
                    expert["now"] = sp.value_load(cell, min_val=0, max_val=TYPES - 1)
                e = expert["now"] + (ffn - NS)
                return experts[bass.ds(e, 1), half].rearrange("o p f -> (o p) f")

            def mixture(b, k, parity, last):
                m = k // 4
                if k % 4 == 0 and not (last and m + 3 >= UNITS):
                    load_wi(b, m + 3)
                if k % 4 == 1 and not (last and m + 3 >= UNITS):
                    load_wo(b, m + 3)

            def beside(step, k, p):
                n, f = p.n, p.f
                if step == "x":
                    if later(n * 2):
                        sp.wait_ge(x2_ready, n * 2)
                    row = x[n] if isinstance(n, int) else x[bass.ds(n, 1)].rearrange("o p f -> (o p) f")
                    sp.dma_start(xt[:, :, :].rearrange("p c t -> p (c t)"), row).then_inc(x_loaded, 16)
                elif step == "mod":
                    sp.wait_ge(mod_ready, n + 1)
                    sp.dma_start(mod_scratch, mod[:, :]).then_inc(mod_stored, 16)
                elif step.startswith("modb"):
                    q = int(step[-1])
                    if q == 0:
                        sp.wait_ge(mod_stored, n * 16 + 16)
                    if q >= 2:
                        sp.wait_ge(ema_in, n * (2 * D) + 4 * (q - 1))
                    sp.dma_start(modb[:, q % 2, :, :], mod_scratch[2 * q:2 * q + 2, :].partition_broadcast(P))\
                        .then_inc(modb_loaded[q % 2], 16)
                elif step == "store":
                    sp.wait_ge(mixed, f * 8 + 8)
                    row = out[f] if isinstance(f, int) else out[bass.ds(f, 1)].rearrange("o p f -> (o p) f")
                    sp.dma_start(row, x2[:, p.f_parity, :, :].rearrange("p c t -> p (c t)")).then_inc(out_stored, 16)

            sp.dma_start(par[:, :], params).then_inc(par_loaded, 16)
            sp.dma_start(y[:, :, :, :].rearrange("p i c t -> p (i c t)")[:, 0:W_ALL], w_ctx[0]).then_inc(wc_loaded, 16)
            sp.dma_start(types_sb[:, :], types_row).then_inc(types_loaded, 16)
            sp.dma_start(types_b[:, :], types_all).then_inc(types_loaded, 16)
            way = drive("sync", mixture, beside)
            sp.dma_start(ident[:, :], w_ctx[1][:, 0:P]).then_inc(ident_loaded, 16)
            sp.wait_ge(types_loaded, 32)
            load_wi(0, 0)
            load_wo(0, 0)
            load_wi(0, 1)
            load_wo(0, 1)
            sp.dma_start(gw1[:, :, :].rearrange("p k e -> p (k e)"), gate_w1).then_inc(gw1_loaded, 16)
            next(way)
            load_wi(0, 2)
            load_wo(0, 2)
            for _ in way:
                pass
            sp.wait_ge(out_stored, B * 16)

        @block.tensor
        def _(pe):
            def product(ps, w_hi, w_lo, x_hi, x_lo, start, stop):
                pe.matmul(ps, w_hi, x_hi, start=start, stop=False)
                pe.matmul(ps, w_hi, x_lo, start=False, stop=False)
                return pe.matmul(ps, w_lo, x_hi, start=False, stop=stop)

            def up(b, k, parity):
                u, j = k // UT, k % UT
                if k == 0:
                    pe.wait_ge(x2_split, b + 1)
                if j == 0:
                    pe.wait_ge(wi_ready, b * UNITS + (u + 1))
                ps = ps_up[k % NU][:, :]
                for c in range(CT):
                    at = slice(c * UF + j * P, c * UF + (j + 1) * P)
                    mm = product(ps, wi_hi[:, u % 2, at], wi_lo[:, u % 2, at], x2_hi[:, parity, c, :],
                                 x2_lo[:, parity, c, :], c == 0, c == CT - 1)
                mm.then_inc(up_done, 1)

            def down(b, k):
                u, j = k // UT, k % UT
                ffn = k // TPF
                if k % TPF == 0:
                    if ffn == 0:
                        if later(b * 2):
                            pe.wait_ge(experts_ready, b * 2)
                    else:
                        pe.wait_ge(y_ready, b * 4 + ffn)
                if j == 0:
                    pe.wait_ge(wo_ready, b * UNITS + (u + 1))
                pe.wait_ge(hid_ready, b * SLOTS + (k + 1))
                for c in range(CT):
                    at = slice(j * E + c * P, j * E + (c + 1) * P)
                    mm = product(ps_down[c][:, :], wo_hi[:, u % 2, at], wo_lo[:, u % 2, at], hid_hi[:, k % NU, :],
                                 hid_lo[:, k % NU, :], k % TPF == 0, k % TPF == TPF - 1)
                mm.then_inc(down_done, 1)

            def mixture(b, k, parity, last):
                if k + LAG < SLOTS:
                    up(b, k + LAG, parity)
                elif not last:
                    up(b + 1, k + LAG - SLOTS, 1 - parity)
                down(b, k)

            def project(p, stage, first, terms):
                for m in range(CT):
                    if later(p.aux[stage]):
                        pe.wait_ge(aux_free[m], p.aux[stage])
                    for i, (w, xh, xl) in enumerate(terms):
                        at = slice(w + m * P, w + (m + 1) * P)
                        mm = product(ps_aux[m][:, :], wc_hi[:, at], wc_lo[:, at], xh, xl, i == 0, i == len(terms) - 1)
                    mm.then_inc(aux_ready[m], 1)

            def beside(step, k, p):
                n, f = p.n, p.f
                x_terms = lambda w: [(w + c * E, xg_hi[:, c, :], xg_lo[:, c, :]) for c in range(CT)]
                c_terms = lambda w: [(w + c * E, ct_hi[:, c, :], ct_lo[:, c, :]) for c in range(CT)]
                if step == "soma":
                    pe.wait_ge(x_ready, n + 1)
                    project(p, "soma", 0, x_terms(W_SOMA))
                elif step == "mod_hidden":
                    if later(p.aux["mod"]):
                        pe.wait_ge(aux_free[0], p.aux["mod"])
                    for c in range(CT):
                        at = slice(W_N1 + c * P, W_N1 + (c + 1) * P)
                        mm = product(ps_aux[0][:, :], wc_hi[:, at], wc_lo[:, at], xg_hi[:, c, :], xg_lo[:, c, :],
                                     c == 0, c == CT - 1)
                    mm.then_inc(aux_ready[0], 1)
                elif step == "mod":
                    pe.wait_ge(modh_split, n + 1)
                    if later(p.aux["mod"]):
                        pe.wait_ge(aux_free[1], p.aux["mod"])
                    at = slice(W_N2, W_N2 + P)
                    product(ps_aux[1][:, :], wc_hi[:, at], wc_lo[:, at], modh_hi[:, :], modh_lo[:, :], True, True)\
                        .then_inc(aux_ready[1], 1)
                elif step == "wgate":
                    pe.wait_ge(ctx_split, n + 1)
                    project(p, "wgate", 0, x_terms(W_GATE) + c_terms(W_GATE + CT * E))
                elif step == "tgate":
                    pe.wait_ge(temp_split, n + 1)
                    project(p, "tgate", 0, c_terms(W_TEMP))
                elif step == "out":
                    pe.wait_ge(sg_split, n + 1)
                    for t in range(TT):
                        bank = t // 2
                        if t % 2 == 0:
                            if later(p.aux["out"]):
                                pe.wait_ge(aux_free[bank], p.aux["out"])
                        for c in range(CT):
                            tok = slice(t * P, (t + 1) * P)
                            at = slice(W_OUT + c * E, W_OUT + (c + 1) * E)
                            mm = product(ps_aux[bank][:, (t % 2) * E:(t % 2 + 1) * E], xg_hi[:, c, tok],
                                         xg_lo[:, c, tok], wc_hi[:, at], wc_lo[:, at], c == 0, c == CT - 1)
                        if t % 2 == 1:
                            mm.then_inc(aux_ready[bank], 1)
                elif step == "turn":
                    pe.wait_ge(normed_ready, n + 1)
                    for c in range(CT):
                        if later(p.aux["turn"]):
                            pe.wait_ge(aux_free[c], p.aux["turn"])
                        for t in range(TT):
                            mm = pe.transpose(ps_aux[c][:, t * P:(t + 1) * P], normed[:, t, c * P:(c + 1) * P], ident[:, :])
                        mm.then_inc(aux_ready[c], 1)
                elif step == "gate_hidden":
                    pe.wait_ge(gate_part, f * 8 + 8)
                    if later(p.aux["gating"]):
                        pe.wait_ge(aux_free[0], p.aux["gating"])
                    for c in range(CT):
                        mm = pe.matmul(ps_aux[0][:, c:c + 1], gpart[:, c * P:(c + 1) * P], ones[:, 0:1],
                                       start=True, stop=True)
                    mm.then_inc(aux_ready[0], 1)
                elif step == "gate_logits":
                    pe.wait_ge(gate_spread, f * 2 + 2)
                    if later(p.aux["gating"]):
                        pe.wait_ge(aux_free[1], p.aux["gating"])
                    for c in range(CT):
                        mm = pe.matmul(ps_aux[1][:, 0:4], gspread[:, c, :], par[:, C_GW2 + 4 * c:C_GW2 + 4 * c + 4],
                                       start=(c == 0), stop=(c == CT - 1))
                    mm.then_inc(aux_ready[1], 1)

            way = drive("tensor", mixture, beside)
            pe.wait_ge(wc_ready, 1)
            pe.wait_ge(ident_loaded, 16)
            pe.wait_ge(par_loaded, 16)
            next(way)
            up(0, 0, 0)
            up(0, 1, 0)
            for _ in way:
                pass

        @block.scalar
        def _(act):
            def hi(out_ap, in_ap):
                return act.activation(out_ap, in_ap, ACT.Copy)

            def both(t):
                return t[:, :, :].rearrange("p c t -> p (c t)")

            def wi_round(b, u):
                b, u, count, buf = unit_of(b, u)
                act.wait_ge(wi_loaded[buf], b * (UNITS // 2 * 16) + 16 * (u // 2 + 1))
                if later(count * UT - UT):
                    act.wait_ge(up_done, count * UT - UT)
                hi(wi_hi[:, buf, :], raw_wi[:, buf, :]).then_inc(wi_hi_ready, 1)

            def wo_round(b, u):
                b, u, count, buf = unit_of(b, u)
                act.wait_ge(wo_loaded[buf], b * (UNITS // 2 * 16) + 16 * (u // 2 + 1))
                if later(count * UT - UT):
                    act.wait_ge(down_done, count * UT - UT)
                hi(wo_hi[:, buf, :], raw_wo[:, buf, :]).then_inc(wo_hi_ready, 1)

            def relu(b, k):
                act.wait_ge(up_done, b * SLOTS + (k + 1))
                if later(b * SLOTS + (k + 1 - NU)):
                    act.wait_ge(down_done, b * SLOTS + (k + 1 - NU))
                act.activation(hid_hi[:, k % NU, :], ps_up[k % NU][:, :], ACT.Relu).then_inc(hid_hi_ready, 1)

            def read_out(b, ffn, b_known):
                act.wait_ge(down_done, b * SLOTS + (ffn + 1) * TPF)
                if ffn == 0:
                    if later(b * 8):
                        act.wait_ge(mixed, b * 8)
                if ffn == NS:
                    act.wait_ge(wa_ready, b + 1)
                for c in range(CT):
                    scale = wa_now[:, 0:1] if ffn == NS else 1.0
                    last = act.activation(y[:, (ffn + 1) % (NS + 1), c, :], ps_down[c][:, :], ACT.Copy, scale=scale)
                last.then_inc(y_ready, 1)

            def mixture(b, k, parity, last):
                if k % TPF == 0 and k > 0:
                    read_out(b, k // TPF - 1, None)
                if k + LAG < SLOTS:
                    relu(b, k + LAG)
                elif not last:
                    relu(b + 1, k + LAG - SLOTS)
                m = k // 4
                if k % 4 == 0 and not (last and m + 1 >= UNITS):
                    wo_round(b, m + 1)
                if k % 4 == 2 and not (last and m + 2 >= UNITS):
                    wi_round(b, m + 2)

            def beside(step, k, p):
                n, f = p.n, p.f
                if step == "x_hi":
                    act.wait_ge(x_loaded, n * 16 + 16)
                    hi(both(xg_hi), both(xt)).then_inc(x_hi_ready, 1)
                elif step == "ctx_hi":
                    act.wait_ge(ctx_ready, n * 2 + 2)
                    hi(both(ct_hi), both(ctxt)).then_inc(ctx_hi_ready, 1)
                elif step == "soma":
                    for c in range(CT):
                        act.wait_ge(aux_ready[c], p.aux["soma"] + 1)
                        act.activation(soma[:, c, :], ps_aux[c][:, :], ACT.Gelu, bias=col(C_BSOMA, c))\
                            .then_inc(aux_free[c], 1)
                elif step == "mod_hidden":
                    act.wait_ge(aux_ready[0], p.aux["mod"] + 1)
                    act.activation(modh[:, :], ps_aux[0][:, :], ACT.Gelu, bias=col(C_BN1)).then_inc(aux_free[0], 1)
                    act.wait_ge(aux_free[0], p.aux["mod"] + 1)
                    hi(modh_hi[:, :], modh[:, :]).then_inc(modh_hi_ready, 1)
                elif step == "mod":
                    act.wait_ge(aux_ready[1], p.aux["mod"] + 1)
                    act.activation(mod[:, :], ps_aux[1][0:D, :], ACT.Sigmoid, bias=par[0:D, C_BN2:C_BN2 + 1])\
                        .then_inc(aux_free[1], 1)
                    act.wait_ge(aux_free[1], p.aux["mod"] + 1)
                    act.nop().then_inc(mod_ready, 1)
                elif step in ("wgate", "tgate"):
                    bias = {"wgate": C_BG, "tgate": C_BTEMP}[step]
                    for c in range(CT):
                        act.wait_ge(aux_ready[c], p.aux[step] + 1)
                        act.activation(gates[:, c, :], ps_aux[c][:, :], ACT.Sigmoid, bias=col(bias, c))\
                            .then_inc(aux_free[c], 1)
                elif step == "temp_hi":
                    act.wait_ge(ema_sum, n * (2 * D) + 2 * D)
                    hi(both(ct_hi), both(temporal)).then_inc(temp_hi_ready, 1)
                elif step == "sg_hi":
                    act.wait_ge(sg_ready, n * 2 + 2)
                    hi(both(xg_hi), both(gates)).then_inc(sg_hi_ready, 1)
                elif step == "ln_sqrt":
                    act.wait_ge(meanvar_ready, n + 1)
                    act.activation(std[:, :], meanvar[:, :, 1], ACT.Sqrt, bias=eps[:, :]).then_inc(std_ready, 1)
                elif step == "turn":
                    if later((n - 1) * 16):
                        act.wait_ge(out_stored, (n - 1) * 16)
                    for c in range(CT):
                        act.wait_ge(aux_ready[c], p.aux["turn"] + 1)
                        act.activation(x2[:, p.n_parity, c, :], ps_aux[c][:, :], ACT.Identity, bias=col(C_BETA, c),
                                       scale=col(C_GAMMA, c)).then_inc(aux_free[c], 1)
                elif step == "x2_hi":
                    act.wait_ge(x2_ready, n * 2 + 2)
                    hi(both(x2_hi[:, p.n_parity, :, :]), both(x2[:, p.n_parity, :, :])).then_inc(x2_hi_ready, 1)
                elif step == "gate_exp":
                    act.wait_ge(aux_ready[1], p.aux["gating"] + 1)
                    act.wait_ge(gate_max, f + 1)
                    act.activation(gexp[:, :], ps_aux[1][:, 0:4], ACT.Exp, bias=gmax[:, :], accum_out=gsum[:, :])\
                        .then_inc(gate_exp, 1)

            way = drive("scalar", mixture, beside)
            act.wait_ge(wc_loaded, 16)
            hi(wc_hi[:, :], y[:, :, :, :].rearrange("p i c t -> p (i c t)")[:, 0:W_ALL]).then_inc(wc_hi_ready, 1)
            act.wait_ge(par_loaded, 16)
            act.activation(alpha[:, :], par[:, C_TAU:C_TAU + D + 1], ACT.Exp).then_inc(alpha_exp, 1)
            act.wait_ge(consts_ready, 1)
            for c in range(CT):
                act.activation(blend_w[:, c, :], par[:, C_BLEND + c * D:C_BLEND + (c + 1) * D], ACT.Exp,
                               bias=soft[:, c:c + 1], accum_out=soft[:, 2 + c:3 + c]).then_inc(alpha_exp, 1)
            for t in range(TYPES):
                act.activation(pairs[:, t, :], par[:, C_GV + t * NE:C_GV + (t + 1) * NE], ACT.Exp,
                               bias=soft[:, 4 + t:5 + t], scale=10.0, accum_out=soft[:, 7 + t:8 + t])\
                    .then_inc(alpha_exp, 1)
            wi_round(0, 0)
            wo_round(0, 0)
            wi_round(0, 1)
            next(way)
            relu(0, 0)
            relu(0, 1)
            for _ in way:
                pass

        @block.vector
        def _(dve):
            def lo(out_ap, in_ap, hi_ap):
                return dve.tensor_tensor(out_ap, in_ap, f32(hi_ap), ALU.subtract)

            def both(t):
                return t[:, :, :].rearrange("p c t -> p (c t)")

            def relu_lo(b, k):
                dve.wait_ge(hid_hi_ready, b * SLOTS + (k + 1))
                dve.scalar_tensor_tensor(hid_lo[:, k % NU, :], ps_up[k % NU][:, :], 0.0, f32(hid_hi[:, k % NU, :]),
                                         ALU.max, ALU.subtract).then_inc(hid_ready, 1)

            def add_expert_b(b):
                dve.wait_ge(down_done, b * SLOTS + SLOTS)
                dve.wait_ge(y_ready, b * 4 + 4)
                for c in range(CT):
                    dve.scalar_tensor_tensor(y[:, 0, c, :], ps_down[c][:, :], wa_now[:, 1:2], y[:, 0, c, :],
                                             ALU.mult, ALU.add).then_inc(experts_ready, 1)

            def pick_weights(b):
                if later(b * 2):
                    dve.wait_ge(experts_ready, b * 2)
                source = wab[:, :, b] if isinstance(b, int) else wab[:, :, bass.ds(b, 1)].rearrange("p a o -> p (a o)")
                dve.tensor_copy(wa_now[:, :], source).then_inc(wa_ready, 1)

            def mixture(b, k, parity, last):
                if k == 0 and not (isinstance(b, int) and b == 0):
                    add_expert_b(b - 1)
                if k + LAG < SLOTS:
                    relu_lo(b, k + LAG)
                elif not last:
                    relu_lo(b + 1, k + LAG - SLOTS)
                if k == 0:
                    pick_weights(b)

            def mix(f, parity, i):
                if i == 0:
                    dve.wait_ge(gate_soft, f * 2 + 2)
                for c in range(CT):
                    if i:
                        dve.wait_ge(mixed, f * 8 + (2 * i - 1 + c))
                    dve.scalar_tensor_tensor(x2[:, parity, c, :], y[:, i, c, :], g[:, i:i + 1], x2[:, parity, c, :],
                                             ALU.mult, ALU.add).then_inc(mixed, 1)

            def beside(step, k, p):
                n, f = p.n, p.f
                if step == "x_lo":
                    dve.wait_ge(x_hi_ready, n + 1)
                    lo(both(xg_lo), both(xt), both(xg_hi)).then_inc(x_ready, 1)
                elif step == "ctx_scan":
                    for c in range(CT):
                        dve.tensor_tensor_scan(ctxt[:, c, :], alpha[:, D:D + 1].broadcast_to([P, T]), xt[:, c, :], 0.0,
                                               ALU.mult, ALU.add).then_inc(ctx_ready, 1)
                elif step == "ctx_lo":
                    dve.wait_ge(ctx_hi_ready, n + 1)
                    lo(both(ct_lo), both(ctxt), both(ct_hi)).then_inc(ctx_split, 1)
                elif step == "mod_hidden_lo":
                    dve.wait_ge(modh_hi_ready, n + 1)
                    lo(modh_lo[:, :], modh[:, :], modh_hi[:, :]).then_inc(modh_split, 1)
                elif step == "gated":
                    for c in range(CT):
                        dve.wait_ge(aux_free[c], p.aux["wgate"] + 1)
                        dve.tensor_tensor(gates[:, c, :], gates[:, c, :], xt[:, c, :], ALU.mult).then_inc(gated_ready, 1)
                elif step.startswith("ema_in"):
                    d = int(step[-1])
                    if d == 0:
                        dve.wait_ge(gated_ready, n * 2 + 2)
                    if d % 2 == 0:
                        dve.wait_ge(modb_loaded[d // 2 % 2], n * 32 + 16 * (d // 4 + 1))
                    for c in range(CT):
                        if d:
                            dve.wait_ge(ema_sum, n * (2 * D) + (2 * d - 1 + c))
                        dve.scalar_tensor_tensor(trace[:, c, :], modb[:, d // 2 % 2, d % 2, :], 0.5, gates[:, c, :],
                                                 ALU.add, ALU.mult).then_inc(ema_in, 1)
                    dve.wait_ge(ema_in, n * (2 * D) + (2 * d + 1))
                    dve.tensor_tensor_scan(trace[:, 0, :], alpha[:, d:d + 1].broadcast_to([P, T]), trace[:, 0, :], 0.0,
                                           ALU.mult, ALU.add).then_inc(ema_trace, 1)
                elif step.startswith("ema_out"):
                    d = int(step[-1])
                    dve.wait_ge(ema_in, n * (2 * D) + (2 * d + 2))
                    dve.tensor_tensor_scan(trace[:, 1, :], alpha[:, d:d + 1].broadcast_to([P, T]), trace[:, 1, :], 0.0,
                                           ALU.mult, ALU.add).then_inc(ema_trace, 1)
                    for c in range(CT):
                        dve.wait_ge(ema_trace, n * (2 * D) + (2 * d + 1 + c))
                        if d == 0:
                            last = dve.tensor_scalar(temporal[:, c, :], trace[:, c, :], blend_w[:, c, 0:1], None, ALU.mult)
                        else:
                            last = dve.scalar_tensor_tensor(temporal[:, c, :], trace[:, c, :], blend_w[:, c, d:d + 1],
                                                            temporal[:, c, :], ALU.mult, ALU.add)
                        last.then_inc(ema_sum, 1)
                elif step == "temp_lo":
                    dve.wait_ge(temp_hi_ready, n + 1)
                    lo(both(ct_lo), both(temporal), both(ct_hi)).then_inc(temp_split, 1)
                elif step == "sg":
                    for c in range(CT):
                        dve.wait_ge(aux_free[c], p.aux["tgate"] + 1)
                        dve.tensor_tensor(gates[:, c, :], gates[:, c, :], soma[:, c, :], ALU.mult).then_inc(sg_ready, 1)
                elif step == "sg_lo":
                    dve.wait_ge(sg_hi_ready, n + 1)
                    lo(both(xg_lo), both(gates), both(xg_hi)).then_inc(sg_split, 1)
                elif step == "ln_stats":
                    for t in range(TT):
                        dve.wait_ge(aux_ready[t // 2], p.aux["out"] + 1)
                        dve.bn_stats(stats[:, t, :], ps_aux[t // 2][:, (t % 2) * E:(t % 2 + 1) * E]).then_inc(stats_ready, 1)
                    dve.wait_ge(stats_ready, n * TT + TT)
                    dve.memset(std[:, :], 0.0)
                    for t in range(TT):
                        last = dve.bn_aggr(meanvar[:, t, :], stats[:, t, :])
                    last.then_inc(meanvar_ready, 1)
                elif step == "ln_norm":
                    dve.wait_ge(std_ready, n + 1)
                    dve.reciprocal(rstd[:, :], std[:, :]).then_inc(rstd_ready, 1)
                    dve.wait_ge(rstd_ready, n + 1)
                    for t in range(TT):
                        last = dve.tensor_scalar(normed[:, t, :], ps_aux[t // 2][:, (t % 2) * E:(t % 2 + 1) * E],
                                                 meanvar[:, t, 0:1], rstd[:, t:t + 1], ALU.subtract, ALU.mult)
                        if t % 2 == 1:
                            last.then_inc(aux_free[t // 2], 1)
                    dve.wait_ge(aux_free[1], p.aux["out"] + 1)
                    dve.nop().then_inc(normed_ready, 1)
                elif step == "x2":
                    for c in range(CT):
                        dve.wait_ge(aux_free[c], p.aux["turn"] + 1)
                        dve.tensor_tensor(x2[:, p.n_parity, c, :], x2[:, p.n_parity, c, :], xt[:, c, :], ALU.add)\
                            .then_inc(x2_ready, 1)
                elif step == "x2_lo":
                    dve.wait_ge(x2_hi_ready, n + 1)
                    lo(both(x2_lo[:, p.n_parity, :, :]), both(x2[:, p.n_parity, :, :]),
                       both(x2_hi[:, p.n_parity, :, :])).then_inc(x2_split, 1)
                elif step == "gate_part":
                    dve.wait_ge(experts_ready, f * 2 + 2)
                    for i, q in enumerate((2, 3, 4, 5, 6, 7, 0, 1)):
                        first = y[:, q // 2, q % 2, 0:1]
                        if i == 0:
                            last = dve.tensor_scalar(gpart[:, :], gw1[:, q, :], first, None, ALU.mult)
                        else:
                            dve.wait_ge(gate_part, f * 8 + i)
                            last = dve.scalar_tensor_tensor(gpart[:, :], gw1[:, q, :], first, gpart[:, :], ALU.mult, ALU.add)
                        last.then_inc(gate_part, 1)
                elif step == "gate_spread":
                    dve.wait_ge(aux_ready[0], p.aux["gating"] + 1)
                    for c in range(CT):
                        last = dve.tensor_scalar(gspread[:, c, :], ones[:, :], ps_aux[0][:, c:c + 1], 0.0, ALU.mult, ALU.max)
                        last.then_inc(gate_spread, 1)
                    dve.wait_ge(gate_spread, f * 2 + 2)
                    dve.nop().then_inc(aux_free[0], 1)
                elif step == "gate_max":
                    dve.wait_ge(aux_ready[1], p.aux["gating"] + 1)
                    dve.tensor_reduce(gmax[:, :], ps_aux[1][:, 0:4], AX_X, ALU.max, negate=True).then_inc(gate_max, 1)
                elif step == "gate_soft":
                    dve.wait_ge(gate_exp, f + 1)
                    dve.reciprocal(grec[:, :], gsum[:, :]).then_inc(gate_soft, 1)
                    dve.wait_ge(gate_soft, f * 2 + 1)
                    dve.tensor_scalar(g[:, :], gexp[:, :], grec[:, :], None, ALU.mult).then_inc(gate_soft, 1)
                    dve.wait_ge(gate_soft, f * 2 + 2)
                    dve.nop().then_inc(aux_free[1], 1)
                elif step == "mix01":
                    mix(f, p.f_parity, 0)
                    mix(f, p.f_parity, 1)
                elif step == "mix2":
                    mix(f, p.f_parity, 2)
                elif step == "mix3":
                    mix(f, p.f_parity, 3)

            done = [0]

            def step(ins):
                done[0] += 1
                ins.then_inc(consts_chain, 1)

            def sync():
                dve.wait_ge(consts_chain, done[0])

            dve.wait_ge(par_loaded, 16)
            step(dve.memset(ones[:, :], 1.0))
            step(dve.memset(eps[:, :], LN_EPS))
            step(dve.tensor_reduce(soft[:, 0:2], par[:, C_BLEND:C_BLEND + CT * D].rearrange("p (c d) -> p c d", c=CT),
                                   AX_X, ALU.max, negate=True))
            step(dve.tensor_reduce(soft[:, 10:13], par[:, C_GV:C_GV + TYPES * NE].rearrange("p (t e) -> p t e", t=TYPES),
                                   AX_X, ALU.max, negate=True))
            sync()
            step(dve.tensor_scalar(soft[:, 4:7], soft[:, 10:13], 10.0, None, ALU.mult))
            sync()
            dve.nop().then_inc(consts_ready, 1)
            dve.wait_ge(types_loaded, 32)
            step(dve.tensor_copy(types_f[:, :], types_b[:, :]))
            dve.wait_ge(alpha_exp, 1 + CT + TYPES)
            step(dve.tensor_scalar(alpha[:, :], alpha[:, :], 1.0, None, ALU.add))
            step(dve.reciprocal(soft[:, 10:15], soft[:, 2:4] if False else soft[:, 2:7]))
            sync()
            step(dve.reciprocal(alpha[:, :], alpha[:, :]))
            for c in range(CT):
                step(dve.tensor_scalar(blend_w[:, c, :], blend_w[:, c, :], soft[:, 10 + c:11 + c], None, ALU.mult))
            dve.wait_ge(wc_hi_ready, 1)
            lo(wc_lo[:, :], y[:, :, :, :].rearrange("p i c t -> p (i c t)")[:, 0:W_ALL], wc_hi[:, :])\
                .then_inc(wc_ready, 1)
            sync()
            step(dve.reciprocal(soft[:, 10:13], soft[:, 7:10]))
            sync()
            for t in range(TYPES):
                for s in range(2):
                    step(dve.tensor_scalar(pairs_s[:, 2 * t + s:2 * t + s + 1], pairs[:, t, t + s:t + s + 1],
                                           soft[:, 10 + t:11 + t], None, ALU.mult))
                step(dve.tensor_scalar(picks[:, t, :], types_f[:, :], float(t), None, ALU.is_equal))
            sync()
            for t in range(TYPES):
                for s in range(2):
                    if t == 0:
                        step(dve.tensor_scalar(wab[:, s, :], picks[:, t, :], pairs_s[:, s:s + 1], None, ALU.mult))
                    else:
                        step(dve.scalar_tensor_tensor(wab[:, s, :], picks[:, t, :], pairs_s[:, 2 * t + s:2 * t + s + 1],
                                                      wab[:, s, :], ALU.mult, ALU.add))
                sync()
            dve.wait_ge(gw1_loaded, 16)

            way = drive("vector", mixture, beside)
            next(way)
            relu_lo(0, 0)
            relu_lo(0, 1)
            next(way)
            add_expert_b(B - 1)
            for _ in way:
                pass

        @block.gpsimd
        def _(pool):
            def wi_rest(b, u):
                b, u, count, buf = unit_of(b, u)
                pool.wait_ge(wi_hi_ready, count + 1)
                pool.tensor_tensor(wi_lo[:, buf, :], raw_wi[:, buf, :], f32(wi_hi[:, buf, :]), ALU.subtract)\
                    .then_inc(wi_ready, 1)

            def wo_rest(b, u):
                b, u, count, buf = unit_of(b, u)
                pool.wait_ge(wo_hi_ready, count + 1)
                pool.tensor_tensor(wo_lo[:, buf, :], raw_wo[:, buf, :], f32(wo_hi[:, buf, :]), ALU.subtract)\
                    .then_inc(wo_ready, 1)

            def mixture(b, k, parity, last):
                m = k // 4
                if k % 4 == 0 and not (last and m + 1 >= UNITS):
                    wo_rest(b, m + 1)
                if k % 4 == 2 and not (last and m + 2 >= UNITS):
                    wi_rest(b, m + 2)

            wi_rest(0, 0)
            wo_rest(0, 0)
            wi_rest(0, 1)
            for _ in drive("gpsimd", mixture, None):
                pass


def kernel(**inputs):
    import concourse.bacc as bacc
    from concourse.bass_utils import run_bass_kernel_spmd

    a = {k: np.asarray(v) for k, v in inputs.items()}

    def rows(w):
        k, n = w.shape[0] // P, w.shape[1]
        return w.reshape(k, P, n).transpose(1, 0, 2).reshape(P, k * n)

    def cols(v):
        return v.reshape(-1, P).T

    def padded(w, r, c):
        out = np.zeros((r, c), np.float32)
        out[:w.shape[0], :w.shape[1]] = w
        return out

    def every(v):
        return np.tile(v.reshape(1, -1), (P, 1))

    w_ctx = np.concatenate([
        rows(a["L0_cond_Wg"].T), rows(a["L0_cond_Wsoma"].T), rows(a["L0_cond_Wtemp"].T), rows(a["L0_cond_Wout"].T),
        rows(padded(a["L0_cond_Wn1"].T, E, P)), padded(a["cond_256"].T, P, P)], axis=1)
    params = np.concatenate([
        cols(a["L0_cond_bg"]), cols(a["L0_cond_bsoma"]), cols(a["L0_cond_btemp"]), cols(a["L0_cond_gamma"]),
        cols(a["L0_cond_beta"]), padded(a["L0_cond_bn1"][:, None], P, 1), padded(a["condB_bn2"][:, None], P, 1),
        a["cond_1024"].reshape(D, CT, P).transpose(2, 1, 0).reshape(P, CT * D),
        every(np.concatenate([a["condB_tauraws"], a["L0_cond_tau_ctx"].reshape(1)])),
        every(a["L1_cond_gate_vecs"]), rows(a["L1_cond_gate_w2"])], axis=1)

    def wi_units(w):
        return w.reshape(-1, CT, P, 2, UF).transpose(0, 3, 2, 1, 4).reshape(-1, 2, P, CT * UF)

    def wo_units(w):
        return w.reshape(-1, 2, UT, P, E).transpose(0, 1, 3, 2, 4).reshape(-1, 2, P, UT * E)

    sent = {
        "x": a["x"].reshape(B, T, CT, P).transpose(0, 3, 2, 1).reshape(B, P, CT * T),
        "w_ctx": np.stack([w_ctx, padded(np.eye(P, dtype=np.float32), P, w_ctx.shape[1])]),
        "params": params,
        "types_row": a["itok_B_0_2"].reshape(1, B),
        "types_all": every(a["itok_B_0_2"]),
        "shared_wi": wi_units(a["L1_cond_share_wi"]),
        "shared_wo": wo_units(a["L1_cond_share_wo"]),
        "expert_wi": wi_units(a["L1_cond_expert_wi"]),
        "expert_wo": wo_units(a["L1_cond_expert_wo"]),
        "gate_w1": rows(a["L1_cond_gate_w1"]),
    }
    nc = bacc.Bacc("TRN2", target_bir_lowering=False, num_devices=1)
    arrays, args = {}, []
    for name, v in sent.items():
        v = np.ascontiguousarray(v)
        arrays[f"in_{name}"] = v
        args.append(nc.dram_tensor(f"in_{name}", v.shape, mybir.dt.from_np(v.dtype), kind="ExternalInput").ap())
    args.append(nc.dram_tensor("out_t", (B, P, CT * T), F32, kind="ExternalOutput").ap())
    build(nc, *args)
    r = run_bass_kernel_spmd(nc, [arrays], core_ids=[0])
    got = np.asarray(r.results[0]["out_t"])
    return np.ascontiguousarray(got.reshape(B, P, CT, T).transpose(0, 3, 2, 1).reshape(B, T, E))
```

```python
from contextlib import ExitStack

import numpy as np

import concourse.bass as bass
from concourse import mybir

ALU = mybir.AluOpType
ACT = mybir.ActivationFunctionType
F32 = mybir.dt.float32
F32R = mybir.dt.float32r
I32 = mybir.dt.int32
AX_X = mybir.AxisListType.X

P = 128
B, T, E = 8, 512, 256
CT = E // P
D = 8
H1 = 64
F = 1024
NE = 4
NS = 3
TYPES = 3
FFNS = NS + 2
UF = F // 2
UT = UF // P
UNITS = FFNS * F // UF
TPF = F // P
SLOTS = FFNS * TPF
LAG = 2
NU = 4
TT = T // P
LN_EPS = 1e-5

W_GATE, W_SOMA, W_TEMP, W_OUT, W_N1, W_N2, W_ALL = np.cumsum(
    [0, 2 * CT * E, CT * E, CT * E, CT * E, CT * P, P]).tolist()
(C_BG, C_BSOMA, C_BTEMP, C_GAMMA, C_BETA, C_BN1, C_BN2, C_BLEND, C_TAU, C_GV, C_GW2, C_ALL) = np.cumsum(
    [0, CT, CT, CT, CT, CT, 1, 1, CT * D, D + 1, TYPES * NE, CT * 4]).tolist()

PLAN_TENSOR = {
    0.5: ["mod_hidden"], 1.5: ["soma"], 2.5: ["mod", "gate_hidden"], 3.5: ["gate_logits"], 4.5: ["wgate"],
    24.5: ["tgate"], 26.5: ["out"], 29.5: ["turn"],
}
PLAN_SCALAR = {
    1: ["mod_hidden"], 2: ["soma"], 3: ["mod"], 4: ["gate_exp"], 5: ["wgate"],
    23.5: ["temp_hi"], 25: ["tgate"], 26: ["sg_hi"], 28: ["ln_sqrt"], 30: ["turn"], 31.5: ["x2_hi"],
    34.5: ["next_x_hi"], 37: ["next_ctx_hi"],
}
PLAN_VECTOR = {
    0.5: ["gate_part"], 1.5: ["mod_hidden_lo"], 3: ["gate_spread"], 4: ["gate_max"],
    4.5: ["gate_soft", "mix1", "mix2"], 5.5: ["mix3"], 6: ["gated"], 6.5: ["mix0"],
    24: ["temp_lo"], 25.5: ["sg"], 26: ["sg_lo"], 27.5: ["ln_stats"], 28.5: ["ln_norm"], 30.5: ["x2"], 32: ["x2_lo"],
    35: ["next_x_lo"], 35.5: ["next_ctx_scan"], 37.5: ["next_ctx_lo"],
}
for _d in range(D):
    PLAN_VECTOR[7.5 + 2 * _d] = [f"ema_in{_d}"]
    PLAN_VECTOR[8.5 + 2 * _d] = [f"ema_out{_d}"]
PLAN_SYNC = {
    3: ["mod"], 4: ["modb0", "modb1"], 8: ["store"], 10: ["modb2"], 14: ["modb3"], 31: ["next_x"],
}
NEXT_SLOT = 33
GATE_PART_SLOT = 33
MIX_ORDER = (1, 2, 3, 0)
AUX_BANKS = {"mod_hidden": (0,), "mod": (1,), "gate_hidden": (0,), "gate_logits": (0,)}
GATING = {"gate_hidden", "gate_logits", "gate_exp", "gate_part", "gate_spread", "gate_max", "gate_soft",
          "mix0", "mix1", "mix2", "mix3", "store"}


def later(count):
    return not isinstance(count, int) or count > 0


class Period:

    def __init__(self, n, f, n_parity, f_parity, aux_before):
        self.n, self.f, self.n_parity, self.f_parity = n, f, n_parity, f_parity
        orders = ([], [])
        for slot in sorted(PLAN_TENSOR):
            for name in self.steps(PLAN_TENSOR, slot):
                for m in AUX_BANKS.get(name, (0, 1)):
                    orders[m].append(name)
        self.aux = [{name: aux_before[m] + i for i, name in enumerate(order)} for m, order in enumerate(orders)]

    def steps(self, plan, slot):
        first_load = isinstance(self.n, int) and self.n < 0
        for name in plan.get(slot, ()):
            if first_load and not name.startswith("next_"):
                continue
            if (self.f if name in GATING else self.n) is not None:
                yield name


def build(nc, x, w_ctx, params, types_row, types_all, shared_wi, shared_wo, expert_wi, expert_wo,
          gate_w1, out):
    mod_scratch = nc.dram_tensor("mod_scratch", [D, T], F32, kind="Internal").ap()

    with ExitStack() as ctx:
        def sb(name, shape, dt=F32):
            return ctx.enter_context(nc.sbuf_tensor(name, shape, dt))

        def sem(name):
            return ctx.enter_context(nc.semaphore(name))

        def sems(name, n):
            return [sem(f"{name}{i}") for i in range(n)]

        raw_wi = sb("raw_wi", [P, 2, CT * UF])
        raw_wo = sb("raw_wo", [P, 2, UT * E])
        wi_hi = sb("wi_hi", [P, 2, CT * UF], F32R)
        wi_lo = sb("wi_lo", [P, 2, CT * UF], F32R)
        wo_hi = sb("wo_hi", [P, 2, UT * E], F32R)
        wo_lo = sb("wo_lo", [P, 2, UT * E], F32R)
        hid_hi = sb("hid_hi", [P, NU, T], F32R)
        hid_lo = sb("hid_lo", [P, NU, T], F32R)
        wc_hi = sb("wc_hi", [P, W_ALL], F32R)
        wc_lo = sb("wc_lo", [P, W_ALL], F32R)
        gw1 = sb("gw1", [P, 8, E])
        par = sb("par", [P, C_ALL])
        types_sb = sb("types_sb", [1, B], I32)
        types_b = sb("types_b", [P, B], I32)
        types_f = sb("types_f", [P, B])
        y = sb("y", [P, 5, CT, T])
        x2 = sb("x2", [P, 2, CT, T])
        x2_hi = sb("x2_hi", [P, 2, CT, T], F32R)
        x2_lo = sb("x2_lo", [P, 2, CT, T], F32R)
        xt = sb("xt", [P, CT, T])
        xg_hi = sb("xg_hi", [P, CT, T], F32R)
        xg_lo = sb("xg_lo", [P, CT, T], F32R)
        ct_hi = sb("ct_hi", [P, CT, T], F32R)
        ct_lo = sb("ct_lo", [P, CT, T], F32R)
        ctxt = sb("ctxt", [P, CT, T])
        temporal = sb("temporal", [P, CT, T])
        soma = sb("soma", [P, CT, T])
        gates = sb("gates", [P, CT, T])
        trace = sb("trace", [P, CT, T])
        modh = sb("modh", [P, T])
        modh_hi = sb("modh_hi", [P, T], F32R)
        modh_lo = sb("modh_lo", [P, T], F32R)
        mod = sb("mod", [D, T])
        modb = sb("modb", [P, 2, 2, T])
        normed = sb("normed", [P, TT, E])
        ident = sb("ident", [P, P])
        ones = sb("ones", [P, P])
        alpha = sb("alpha", [P, D + 1])
        blend_w = sb("blend_w", [P, CT, D])
        soft = sb("soft", [P, 16])
        pairs = sb("pairs", [P, TYPES, NE])
        pairs_s = sb("pairs_s", [P, 2 * TYPES])
        wab = sb("wab", [P, 2, B])
        picks = sb("picks", [P, TYPES, B])
        wa_now = sb("wa_now", [P, 2])
        gpart = sb("gpart", [P, E])
        gspread = sb("gspread", [P, CT, P])
        gmax = sb("gmax", [P, 1])
        gexp = sb("gexp", [P, 4])
        gsig = sb("gsig", [P, 4])
        gsum = sb("gsum", [P, 1])
        grec = sb("grec", [P, 1])
        g = sb("g", [P, 4])
        stats = sb("stats", [P, TT, 6])
        meanvar = sb("meanvar", [P, TT, 2])
        std = sb("std", [P, TT])
        rstd = sb("rstd", [P, TT])
        eps = sb("eps", [P, 1])

        ps_up = [ctx.enter_context(nc.psum_tensor(f"ps_up{i}", [P, T], F32)) for i in range(NU)]
        ps_down = [ctx.enter_context(nc.psum_tensor(f"ps_down{i}", [P, T], F32)) for i in range(CT)]
        ps_aux = [ctx.enter_context(nc.psum_tensor(f"ps_aux{i}", [P, T], F32)) for i in range(2)]

        par_loaded = sem("par_loaded")
        types_loaded = sem("types_loaded")
        wc_loaded = sem("wc_loaded")
        ident_loaded = sem("ident_loaded")
        consts_ready = sem("consts_ready")
        consts_chain = sem("consts_chain")
        alpha_exp = sem("alpha_exp")
        wc_hi_ready = sem("wc_hi_ready")
        wc_ready = sem("wc_ready")
        wi_loaded = sems("wi_loaded", 2)
        wo_loaded = sems("wo_loaded", 2)
        wi_hi_ready = sem("wi_hi_ready")
        wo_hi_ready = sem("wo_hi_ready")
        wi_ready = sem("wi_ready")
        wo_ready = sem("wo_ready")
        up_done = sem("up_done")
        hid_hi_ready = sem("hid_hi_ready")
        hid_ready = sem("hid_ready")
        down_done = sem("down_done")
        y_ready = sem("y_ready")
        experts_ready = sem("experts_ready")
        aux_ready = sems("aux_ready", 2)
        aux_free = sems("aux_free", 2)
        x_loaded = sem("x_loaded")
        x_hi_ready = sem("x_hi_ready")
        x_ready = sem("x_ready")
        ctx_ready = sem("ctx_ready")
        ctx_hi_ready = sem("ctx_hi_ready")
        ctx_split = sem("ctx_split")
        soma_ready = sem("soma_ready")
        modh_ready = sem("modh_ready")
        modh_hi_ready = sem("modh_hi_ready")
        modh_split = sem("modh_split")
        mod_ready = sem("mod_ready")
        mod_stored = sem("mod_stored")
        modb_loaded = sems("modb_loaded", 2)
        wgate_ready = sem("wgate_ready")
        gated_ready = sem("gated_ready")
        ema_in = sem("ema_in")
        ema_trace = sem("ema_trace")
        ema_sum = sem("ema_sum")
        temp_hi_ready = sem("temp_hi_ready")
        temp_split = sem("temp_split")
        tgate_ready = sem("tgate_ready")
        sg_ready = sem("sg_ready")
        sg_hi_ready = sem("sg_hi_ready")
        sg_split = sem("sg_split")
        stats_ready = sem("stats_ready")
        meanvar_ready = sem("meanvar_ready")
        std_ready = sem("std_ready")
        rstd_ready = sem("rstd_ready")
        normed_ready = sem("normed_ready")
        turned_ready = sem("turned_ready")
        x2_ready = sem("x2_ready")
        x2_hi_ready = sem("x2_hi_ready")
        x2_split = sem("x2_split")
        gate_part = sem("gate_part")
        gate_spread = sem("gate_spread")
        gate_max = sem("gate_max")
        gate_soft = sem("gate_soft")
        mixed = sem("mixed")
        wa_ready = sem("wa_ready")
        out_stored = sem("out_stored")
        gw1_loaded = sem("gw1_loaded")

        def f32(ap):
            return ap.bitcast(F32)

        def y_at(i, parity):
            return 4 if i == 1 and parity else i

        def col(c, i=0):
            return par[:, c + i:c + i + 1]

        def drive(eng, mixture, beside):
            ctx_uses, gating_uses = (6, 6), (2, 0)
            both_uses = [ctx_uses[m] + gating_uses[m] for m in range(2)]

            def p_steps(p, k):
                return list(p.steps(PLANS[eng], k))

            def alone(p, slots):
                for k in slots:
                    for s in p_steps(p, k) + p_steps(p, k + 0.5):
                        beside(s, k, p)

            def run(b, parity, p, last):
                for k in range(SLOTS):
                    for s in p_steps(p, k):
                        beside(s, k, p)
                    mixture(b, k, parity, last)
                    for s in p_steps(p, k + 0.5):
                        beside(s, k, p)

            alone(Period(-1, None, 1, None, (0, 0)), range(SLOTS))
            alone(Period(0, None, 0, None, (0, 0)), range(NEXT_SLOT))
            yield "mixture starts"
            alone(Period(0, None, 0, None, (0, 0)), range(NEXT_SLOT, SLOTS))
            run(0, 0, Period(1, None, 1, None, ctx_uses), False)
            pairs_of_batches = (B - 2) // 2
            with ENGINES[eng].Fori(0, pairs_of_batches) as i:
                for j in range(2):
                    b = i * 2 + (1 + j)
                    p = Period(i * 2 + (2 + j), i * 2 + j, j % 2, j % 2,
                               [i * (2 * both_uses[m]) + (2 * ctx_uses[m] + j * both_uses[m]) for m in range(2)])
                    run(b, (1 + j) % 2, p, False)
            before = [2 * ctx_uses[m] + (B - 2) * both_uses[m] for m in range(2)]
            after = [before[m] + gating_uses[m] for m in range(2)]
            run(B - 1, 1, Period(None, B - 2, None, 0, before), True)
            yield "mixture ends"
            alone(Period(None, B - 1, None, 1, after), range(SLOTS))

        block = ctx.enter_context(nc.Block())
        PLANS = {"sync": PLAN_SYNC, "tensor": PLAN_TENSOR, "scalar": PLAN_SCALAR, "vector": PLAN_VECTOR,
                 "gpsimd": {}}
        ENGINES = {"sync": nc.sync, "tensor": nc.tensor, "scalar": nc.scalar, "vector": nc.vector,
                   "gpsimd": nc.gpsimd}

        def unit_of(b, u):
            if u >= UNITS:
                b, u = b + 1, u - UNITS
            return b, u, b * UNITS + u, u % 2

        @block.sync
        def _(sp):
            expert = {}

            def load_wi(b, u):
                b, u, count, buf = unit_of(b, u)
                if later(count - 1):
                    sp.wait_ge(wi_ready, count - 1)
                sp.dma_start(raw_wi[:, buf, :], source(shared_wi, expert_wi, b, u)).then_inc(wi_loaded[buf], 16)

            def load_wo(b, u):
                b, u, count, buf = unit_of(b, u)
                if later(count - 1):
                    sp.wait_ge(wo_ready, count - 1)
                sp.dma_start(raw_wo[:, buf, :], source(shared_wo, expert_wo, b, u)).then_inc(wo_loaded[buf], 16)

            def source(shared, experts, b, u):
                ffn, half = u // 2, u % 2
                if ffn < NS:
                    return shared[ffn, half]
                if (ffn, half) == (NS, 0) and shared is shared_wi:
                    at = b if isinstance(b, int) else bass.ds(b, 1)
                    cell = types_sb[0:1, b:b + 1] if isinstance(b, int) else types_sb[0:1, at]
                    expert["now"] = sp.value_load(cell, min_val=0, max_val=TYPES - 1)
                e = expert["now"] + (ffn - NS)
                return experts[bass.ds(e, 1), half].rearrange("o p f -> (o p) f")

            def mixture(b, k, parity, last):
                m = k // 4
                if k % 4 == 0 and not (last and m + 3 >= UNITS):
                    load_wi(b, m + 3)
                if k % 4 == 1 and not (last and m + 3 >= UNITS):
                    load_wo(b, m + 3)

            def beside(step, k, p):
                n, f = p.n, p.f
                if step == "next_x":
                    m = n + 1
                    if later(m * 2):
                        sp.wait_ge(x2_ready, m * 2)
                    row = x[m] if isinstance(m, int) else x[bass.ds(m, 1)].rearrange("o p f -> (o p) f")
                    sp.dma_start(xt[:, :, :].rearrange("p c t -> p (c t)"), row).then_inc(x_loaded, 16)
                elif step == "mod":
                    sp.wait_ge(mod_ready, n + 1)
                    sp.dma_start(mod_scratch, mod[:, :]).then_inc(mod_stored, 16)
                elif step.startswith("modb"):
                    q = int(step[-1])
                    if q == 0:
                        sp.wait_ge(mod_stored, n * 16 + 16)
                    if q >= 2:
                        sp.wait_ge(ema_in, n * (2 * D) + 4 * (q - 1))
                    sp.dma_start(modb[:, q % 2, :, :], mod_scratch[2 * q:2 * q + 2, :].partition_broadcast(P))\
                        .then_inc(modb_loaded[q % 2], 16)
                elif step == "store":
                    sp.wait_ge(mixed, f * 8 + 8)
                    row = out[f] if isinstance(f, int) else out[bass.ds(f, 1)].rearrange("o p f -> (o p) f")
                    sp.dma_start(row, x2[:, p.f_parity, :, :].rearrange("p c t -> p (c t)")).then_inc(out_stored, 16)

            sp.dma_start(par[:, :], params).then_inc(par_loaded, 16)
            sp.dma_start(y[:, :, :, :].rearrange("p i c t -> p (i c t)")[:, 0:W_ALL], w_ctx[0]).then_inc(wc_loaded, 16)
            sp.dma_start(types_sb[:, :], types_row).then_inc(types_loaded, 16)
            sp.dma_start(types_b[:, :], types_all).then_inc(types_loaded, 16)
            way = drive("sync", mixture, beside)
            sp.dma_start(ident[:, :], w_ctx[1][:, 0:P]).then_inc(ident_loaded, 16)
            sp.wait_ge(types_loaded, 32)
            load_wi(0, 0)
            load_wo(0, 0)
            load_wi(0, 1)
            load_wo(0, 1)
            sp.dma_start(gw1[:, :, :].rearrange("p k e -> p (k e)"), gate_w1).then_inc(gw1_loaded, 16)
            next(way)
            load_wi(0, 2)
            load_wo(0, 2)
            for _ in way:
                pass
            sp.wait_ge(out_stored, B * 16)

        @block.tensor
        def _(pe):
            def product(ps, w_hi, w_lo, x_hi, x_lo, start, stop):
                pe.matmul(ps, w_hi, x_hi, start=start, stop=False)
                pe.matmul(ps, w_hi, x_lo, start=False, stop=False)
                return pe.matmul(ps, w_lo, x_hi, start=False, stop=stop)

            def up(b, k, parity):
                u, j = k // UT, k % UT
                if k == 0:
                    pe.wait_ge(x2_split, b + 1)
                if j == 0:
                    pe.wait_ge(wi_ready, b * UNITS + (u + 1))
                ps = ps_up[k % NU][:, :]
                for c in range(CT):
                    at = slice(c * UF + j * P, c * UF + (j + 1) * P)
                    mm = product(ps, wi_hi[:, u % 2, at], wi_lo[:, u % 2, at], x2_hi[:, parity, c, :],
                                 x2_lo[:, parity, c, :], c == 0, c == CT - 1)
                mm.then_inc(up_done, 1)

            def down(b, k):
                u, j = k // UT, k % UT
                ffn = k // TPF
                if j == 0:
                    pe.wait_ge(wo_ready, b * UNITS + (u + 1))
                pe.wait_ge(hid_ready, b * SLOTS + (k + 1))
                for c in range(CT):
                    at = slice(j * E + c * P, j * E + (c + 1) * P)
                    if k % TPF == 0 and ffn == 0 and later(b * 2):
                        pe.wait_ge(experts_ready, b * 2 - (1 - c))
                    if k % TPF == 0 and ffn > 0:
                        pe.wait_ge(y_ready, b * 8 + (2 * ffn - 1 + c))
                    mm = product(ps_down[c][:, :], wo_hi[:, u % 2, at], wo_lo[:, u % 2, at], hid_hi[:, k % NU, :],
                                 hid_lo[:, k % NU, :], k % TPF == 0, k % TPF == TPF - 1)
                mm.then_inc(down_done, 1)

            def mixture(b, k, parity, last):
                if k + LAG < SLOTS:
                    up(b, k + LAG, parity)
                elif not last:
                    up(b + 1, k + LAG - SLOTS, 1 - parity)
                down(b, k)

            def project(p, stage, first, terms):
                for m in range(CT):
                    if later(p.aux[m][stage]):
                        pe.wait_ge(aux_free[m], p.aux[m][stage])
                    for i, (w, xh, xl) in enumerate(terms):
                        at = slice(w + m * P, w + (m + 1) * P)
                        mm = product(ps_aux[m][:, :], wc_hi[:, at], wc_lo[:, at], xh, xl, i == 0, i == len(terms) - 1)
                    mm.then_inc(aux_ready[m], 1)

            def beside(step, k, p):
                n, f = p.n, p.f
                x_terms = lambda w: [(w + c * E, xg_hi[:, c, :], xg_lo[:, c, :]) for c in range(CT)]
                c_terms = lambda w: [(w + c * E, ct_hi[:, c, :], ct_lo[:, c, :]) for c in range(CT)]
                if step == "soma":
                    project(p, "soma", 0, x_terms(W_SOMA))
                elif step == "mod_hidden":
                    pe.wait_ge(x_ready, n + 1)
                    if later(p.aux[0]["mod_hidden"]):
                        pe.wait_ge(aux_free[0], p.aux[0]["mod_hidden"])
                    for c in range(CT):
                        at = slice(W_N1 + c * P, W_N1 + (c + 1) * P)
                        mm = product(ps_aux[0][:, :], wc_hi[:, at], wc_lo[:, at], xg_hi[:, c, :], xg_lo[:, c, :],
                                     c == 0, c == CT - 1)
                    mm.then_inc(aux_ready[0], 1)
                elif step == "mod":
                    pe.wait_ge(modh_split, n + 1)
                    if later(p.aux[1]["mod"]):
                        pe.wait_ge(aux_free[1], p.aux[1]["mod"])
                    at = slice(W_N2, W_N2 + P)
                    product(ps_aux[1][:, :], wc_hi[:, at], wc_lo[:, at], modh_hi[:, :], modh_lo[:, :], True, True)\
                        .then_inc(aux_ready[1], 1)
                elif step == "wgate":
                    pe.wait_ge(ctx_split, n + 1)
                    project(p, "wgate", 0, x_terms(W_GATE) + c_terms(W_GATE + CT * E))
                elif step == "tgate":
                    pe.wait_ge(temp_split, n + 1)
                    project(p, "tgate", 0, c_terms(W_TEMP))
                elif step == "out":
                    pe.wait_ge(sg_split, n + 1)
                    for t in range(TT):
                        bank = t // 2
                        if t % 2 == 0:
                            if later(p.aux[bank]["out"]):
                                pe.wait_ge(aux_free[bank], p.aux[bank]["out"])
                        for c in range(CT):
                            tok = slice(t * P, (t + 1) * P)
                            at = slice(W_OUT + c * E, W_OUT + (c + 1) * E)
                            mm = product(ps_aux[bank][:, (t % 2) * E:(t % 2 + 1) * E], xg_hi[:, c, tok],
                                         xg_lo[:, c, tok], wc_hi[:, at], wc_lo[:, at], c == 0, c == CT - 1)
                        if t % 2 == 1:
                            mm.then_inc(aux_ready[bank], 1)
                elif step == "turn":
                    pe.wait_ge(normed_ready, n + 1)
                    for c in range(CT):
                        if later(p.aux[c]["turn"]):
                            pe.wait_ge(aux_free[c], p.aux[c]["turn"])
                        for t in range(TT):
                            mm = pe.transpose(ps_aux[c][:, t * P:(t + 1) * P], normed[:, t, c * P:(c + 1) * P], ident[:, :])
                        mm.then_inc(aux_ready[c], 1)
                elif step == "gate_hidden":
                    pe.wait_ge(gate_part, f * 8 + 8)
                    if later(p.aux[0]["gate_hidden"]):
                        pe.wait_ge(aux_free[0], p.aux[0]["gate_hidden"])
                    for c in range(CT):
                        mm = pe.matmul(ps_aux[0][:, c:c + 1], gpart[:, c * P:(c + 1) * P], ones[:, 0:1],
                                       start=True, stop=True)
                    mm.then_inc(aux_ready[0], 1)
                elif step == "gate_logits":
                    pe.wait_ge(gate_spread, f * 2 + 2)
                    if later(p.aux[0]["gate_logits"]):
                        pe.wait_ge(aux_free[0], p.aux[0]["gate_logits"])
                    for c in range(CT):
                        mm = pe.matmul(ps_aux[0][:, 0:4], gspread[:, c, :], par[:, C_GW2 + 4 * c:C_GW2 + 4 * c + 4],
                                       start=(c == 0), stop=(c == CT - 1))
                    mm.then_inc(aux_ready[0], 1)

            way = drive("tensor", mixture, beside)
            pe.wait_ge(wc_ready, 1)
            pe.wait_ge(ident_loaded, 16)
            pe.wait_ge(par_loaded, 16)
            next(way)
            up(0, 0, 0)
            up(0, 1, 0)
            for _ in way:
                pass

        @block.scalar
        def _(act):
            def hi(out_ap, in_ap):
                return act.activation(out_ap, in_ap, ACT.Copy)

            def both(t):
                return t[:, :, :].rearrange("p c t -> p (c t)")

            def wi_round(b, u):
                b, u, count, buf = unit_of(b, u)
                act.wait_ge(wi_loaded[buf], b * (UNITS // 2 * 16) + 16 * (u // 2 + 1))
                if later(count * UT - UT):
                    act.wait_ge(up_done, count * UT - UT)
                hi(wi_hi[:, buf, :], raw_wi[:, buf, :]).then_inc(wi_hi_ready, 1)

            def wo_round(b, u):
                b, u, count, buf = unit_of(b, u)
                act.wait_ge(wo_loaded[buf], b * (UNITS // 2 * 16) + 16 * (u // 2 + 1))
                if later(count * UT - UT):
                    act.wait_ge(down_done, count * UT - UT)
                hi(wo_hi[:, buf, :], raw_wo[:, buf, :]).then_inc(wo_hi_ready, 1)

            def relu(b, k):
                act.wait_ge(up_done, b * SLOTS + (k + 1))
                if later(b * SLOTS + (k + 1 - NU)):
                    act.wait_ge(down_done, b * SLOTS + (k + 1 - NU))
                act.activation(hid_hi[:, k % NU, :], ps_up[k % NU][:, :], ACT.Relu).then_inc(hid_hi_ready, 1)

            def read_out(b, ffn, parity):
                act.wait_ge(down_done, b * SLOTS + (ffn + 1) * TPF)
                if later(b * 8):
                    act.wait_ge(mixed, (b - 1) * 8 + (2 * ffn + 2 if ffn else 0))
                if ffn == NS:
                    act.wait_ge(wa_ready, b + 1)
                for c in range(CT):
                    scale = wa_now[:, 0:1] if ffn == NS else 1.0
                    act.activation(y[:, y_at((ffn + 1) % (NS + 1), parity), c, :], ps_down[c][:, :], ACT.Copy, scale=scale)\
                        .then_inc(y_ready, 1)

            def mixture(b, k, parity, last):
                if k % TPF == 0 and k > 0:
                    read_out(b, k // TPF - 1, parity)
                if k + LAG < SLOTS:
                    relu(b, k + LAG)
                elif not last:
                    relu(b + 1, k + LAG - SLOTS)
                m = k // 4
                if k % 4 == 0 and not (last and m + 1 >= UNITS):
                    wo_round(b, m + 1)
                if k % 4 == 2 and not (last and m + 2 >= UNITS):
                    wi_round(b, m + 2)

            def beside(step, k, p):
                n, f = p.n, p.f
                if step == "next_x_hi":
                    act.wait_ge(x_loaded, (n + 1) * 16 + 16)
                    hi(both(xg_hi), both(xt)).then_inc(x_hi_ready, 1)
                elif step == "next_ctx_hi":
                    act.wait_ge(ctx_ready, (n + 1) * 2 + 2)
                    hi(both(ct_hi), both(ctxt)).then_inc(ctx_hi_ready, 1)
                elif step == "soma":
                    for c in range(CT):
                        act.wait_ge(aux_ready[c], p.aux[c]["soma"] + 1)
                        act.activation(soma[:, c, :], ps_aux[c][:, :], ACT.Gelu, bias=col(C_BSOMA, c))\
                            .then_inc(aux_free[c], 1)
                elif step == "mod_hidden":
                    act.wait_ge(aux_ready[0], p.aux[0]["mod_hidden"] + 1)
                    act.activation(modh[:, :], ps_aux[0][:, :], ACT.Gelu, bias=col(C_BN1)).then_inc(aux_free[0], 1)
                    act.wait_ge(aux_free[0], p.aux[0]["mod_hidden"] + 1)
                    hi(modh_hi[:, :], modh[:, :]).then_inc(modh_hi_ready, 1)
                elif step == "mod":
                    act.wait_ge(aux_ready[1], p.aux[1]["mod"] + 1)
                    act.activation(mod[:, :], ps_aux[1][0:D, :], ACT.Sigmoid, bias=par[0:D, C_BN2:C_BN2 + 1])\
                        .then_inc(aux_free[1], 1)
                    act.wait_ge(aux_free[1], p.aux[1]["mod"] + 1)
                    act.nop().then_inc(mod_ready, 1)
                elif step in ("wgate", "tgate"):
                    bias = {"wgate": C_BG, "tgate": C_BTEMP}[step]
                    for c in range(CT):
                        act.wait_ge(aux_ready[c], p.aux[c][step] + 1)
                        act.activation(gates[:, c, :], ps_aux[c][:, :], ACT.Sigmoid, bias=col(bias, c))\
                            .then_inc(aux_free[c], 1)
                elif step == "temp_hi":
                    act.wait_ge(ema_sum, n * (2 * D) + 2 * D)
                    hi(both(ct_hi), both(temporal)).then_inc(temp_hi_ready, 1)
                elif step == "sg_hi":
                    act.wait_ge(sg_ready, n * 2 + 2)
                    hi(both(xg_hi), both(gates)).then_inc(sg_hi_ready, 1)
                elif step == "ln_sqrt":
                    act.wait_ge(meanvar_ready, n + 1)
                    act.activation(std[:, :], meanvar[:, :, 1], ACT.Sqrt, bias=eps[:, :]).then_inc(std_ready, 1)
                elif step == "turn":
                    if later((n - 1) * 16):
                        act.wait_ge(out_stored, (n - 1) * 16)
                    for c in range(CT):
                        act.wait_ge(aux_ready[c], p.aux[c]["turn"] + 1)
                        act.activation(x2[:, p.n_parity, c, :], ps_aux[c][:, :], ACT.Identity, bias=col(C_BETA, c),
                                       scale=col(C_GAMMA, c)).then_inc(aux_free[c], 1)
                elif step == "x2_hi":
                    act.wait_ge(x2_ready, n * 2 + 2)
                    hi(both(x2_hi[:, p.n_parity, :, :]), both(x2[:, p.n_parity, :, :])).then_inc(x2_hi_ready, 1)
                elif step == "gate_exp":
                    act.wait_ge(aux_ready[0], p.aux[0]["gate_logits"] + 1)
                    act.wait_ge(gate_max, f + 1)
                    act.activation(gsig[:, :], ps_aux[0][:, 0:4], ACT.Sigmoid, bias=gmax[:, :]).then_inc(aux_free[0], 1)

            way = drive("scalar", mixture, beside)
            act.wait_ge(wc_loaded, 16)
            hi(wc_hi[:, :], y[:, :, :, :].rearrange("p i c t -> p (i c t)")[:, 0:W_ALL]).then_inc(wc_hi_ready, 1)
            act.wait_ge(par_loaded, 16)
            act.activation(alpha[:, :], par[:, C_TAU:C_TAU + D + 1], ACT.Exp).then_inc(alpha_exp, 1)
            act.wait_ge(consts_ready, 1)
            for c in range(CT):
                act.activation(blend_w[:, c, :], par[:, C_BLEND + c * D:C_BLEND + (c + 1) * D], ACT.Exp,
                               bias=soft[:, c:c + 1], accum_out=soft[:, 2 + c:3 + c]).then_inc(alpha_exp, 1)
            for t in range(TYPES):
                act.activation(pairs[:, t, :], par[:, C_GV + t * NE:C_GV + (t + 1) * NE], ACT.Exp,
                               bias=soft[:, 4 + t:5 + t], scale=10.0, accum_out=soft[:, 7 + t:8 + t])\
                    .then_inc(alpha_exp, 1)
            wi_round(0, 0)
            wo_round(0, 0)
            wi_round(0, 1)
            next(way)
            relu(0, 0)
            relu(0, 1)
            for _ in way:
                pass

        @block.vector
        def _(dve):
            def lo(out_ap, in_ap, hi_ap):
                return dve.tensor_tensor(out_ap, in_ap, f32(hi_ap), ALU.subtract)

            def both(t):
                return t[:, :, :].rearrange("p c t -> p (c t)")

            def relu_lo(b, k):
                dve.wait_ge(hid_hi_ready, b * SLOTS + (k + 1))
                dve.scalar_tensor_tensor(hid_lo[:, k % NU, :], ps_up[k % NU][:, :], 0.0, f32(hid_hi[:, k % NU, :]),
                                         ALU.max, ALU.subtract).then_inc(hid_ready, 1)

            def add_expert_b(b):
                dve.wait_ge(down_done, b * SLOTS + SLOTS)
                dve.wait_ge(y_ready, b * 8 + 8)
                for c in range(CT):
                    dve.scalar_tensor_tensor(y[:, 0, c, :], ps_down[c][:, :], wa_now[:, 1:2], y[:, 0, c, :],
                                             ALU.mult, ALU.add).then_inc(experts_ready, 1)

            def pick_weights(b):
                if later(b * 2):
                    dve.wait_ge(experts_ready, b * 2)
                source = wab[:, :, b] if isinstance(b, int) else wab[:, :, bass.ds(b, 1)].rearrange("p a o -> p (a o)")
                dve.tensor_copy(wa_now[:, :], source).then_inc(wa_ready, 1)

            def shared_gate_part(b, parity):
                dve.wait_ge(y_ready, b * 8 + 6)
                for i, q in enumerate((2, 3, 4, 5, 6, 7)):
                    first = y[:, y_at(q // 2, parity), q % 2, 0:1]
                    if i == 0:
                        last = dve.tensor_scalar(gpart[:, :], gw1[:, q, :], first, None, ALU.mult)
                    else:
                        dve.wait_ge(gate_part, b * 8 + i)
                        last = dve.scalar_tensor_tensor(gpart[:, :], gw1[:, q, :], first, gpart[:, :], ALU.mult, ALU.add)
                    last.then_inc(gate_part, 1)

            def mixture(b, k, parity, last):
                if k == 0 and not (isinstance(b, int) and b == 0):
                    add_expert_b(b - 1)
                if k + LAG < SLOTS:
                    relu_lo(b, k + LAG)
                elif not last:
                    relu_lo(b + 1, k + LAG - SLOTS)
                if k == 0:
                    pick_weights(b)
                if k == GATE_PART_SLOT:
                    shared_gate_part(b, parity)

            def mix(f, parity, i):
                at = MIX_ORDER.index(i)
                if at == 0:
                    dve.wait_ge(gate_soft, f * 6 + 6)
                for c in range(CT):
                    if at:
                        dve.wait_ge(mixed, f * 8 + (2 * at - 1 + c))
                    dve.scalar_tensor_tensor(x2[:, parity, c, :], y[:, y_at(i, parity), c, :], g[:, i:i + 1], x2[:, parity, c, :],
                                             ALU.mult, ALU.add).then_inc(mixed, 1)

            def beside(step, k, p):
                n, f = p.n, p.f
                if step == "next_x_lo":
                    dve.wait_ge(x_hi_ready, (n + 1) + 1)
                    lo(both(xg_lo), both(xt), both(xg_hi)).then_inc(x_ready, 1)
                elif step == "next_ctx_scan":
                    for c in range(CT):
                        dve.tensor_tensor_scan(ctxt[:, c, :], alpha[:, D:D + 1].broadcast_to([P, T]), xt[:, c, :], 0.0,
                                               ALU.mult, ALU.add).then_inc(ctx_ready, 1)
                elif step == "next_ctx_lo":
                    dve.wait_ge(ctx_hi_ready, (n + 1) + 1)
                    lo(both(ct_lo), both(ctxt), both(ct_hi)).then_inc(ctx_split, 1)
                elif step == "mod_hidden_lo":
                    dve.wait_ge(modh_hi_ready, n + 1)
                    lo(modh_lo[:, :], modh[:, :], modh_hi[:, :]).then_inc(modh_split, 1)
                elif step == "gated":
                    for c in range(CT):
                        dve.wait_ge(aux_free[c], p.aux[c]["wgate"] + 1)
                        dve.tensor_tensor(gates[:, c, :], gates[:, c, :], xt[:, c, :], ALU.mult).then_inc(gated_ready, 1)
                elif step.startswith("ema_in"):
                    d = int(step[-1])
                    if d == 0:
                        dve.wait_ge(gated_ready, n * 2 + 2)
                    if d % 2 == 0:
                        dve.wait_ge(modb_loaded[d // 2 % 2], n * 32 + 16 * (d // 4 + 1))
                    for c in range(CT):
                        if d:
                            dve.wait_ge(ema_sum, n * (2 * D) + (2 * d - 1 + c))
                        dve.scalar_tensor_tensor(trace[:, c, :], modb[:, d // 2 % 2, d % 2, :], 0.5, gates[:, c, :],
                                                 ALU.add, ALU.mult).then_inc(ema_in, 1)
                    dve.wait_ge(ema_in, n * (2 * D) + (2 * d + 1))
                    dve.tensor_tensor_scan(trace[:, 0, :], alpha[:, d:d + 1].broadcast_to([P, T]), trace[:, 0, :], 0.0,
                                           ALU.mult, ALU.add).then_inc(ema_trace, 1)
                elif step.startswith("ema_out"):
                    d = int(step[-1])
                    dve.wait_ge(ema_in, n * (2 * D) + (2 * d + 2))
                    dve.tensor_tensor_scan(trace[:, 1, :], alpha[:, d:d + 1].broadcast_to([P, T]), trace[:, 1, :], 0.0,
                                           ALU.mult, ALU.add).then_inc(ema_trace, 1)
                    for c in range(CT):
                        dve.wait_ge(ema_trace, n * (2 * D) + (2 * d + 1 + c))
                        if d == 0:
                            last = dve.tensor_scalar(temporal[:, c, :], trace[:, c, :], blend_w[:, c, 0:1], None, ALU.mult)
                        else:
                            last = dve.scalar_tensor_tensor(temporal[:, c, :], trace[:, c, :], blend_w[:, c, d:d + 1],
                                                            temporal[:, c, :], ALU.mult, ALU.add)
                        last.then_inc(ema_sum, 1)
                elif step == "temp_lo":
                    dve.wait_ge(temp_hi_ready, n + 1)
                    lo(both(ct_lo), both(temporal), both(ct_hi)).then_inc(temp_split, 1)
                elif step == "sg":
                    for c in range(CT):
                        dve.wait_ge(aux_free[c], p.aux[c]["tgate"] + 1)
                        dve.tensor_tensor(gates[:, c, :], gates[:, c, :], soma[:, c, :], ALU.mult).then_inc(sg_ready, 1)
                elif step == "sg_lo":
                    dve.wait_ge(sg_hi_ready, n + 1)
                    lo(both(xg_lo), both(gates), both(xg_hi)).then_inc(sg_split, 1)
                elif step == "ln_stats":
                    for t in range(TT):
                        dve.wait_ge(aux_ready[t // 2], p.aux[t // 2]["out"] + 1)
                        dve.bn_stats(stats[:, t, :], ps_aux[t // 2][:, (t % 2) * E:(t % 2 + 1) * E]).then_inc(stats_ready, 1)
                    dve.wait_ge(stats_ready, n * TT + TT)
                    dve.memset(std[:, :], 0.0)
                    for t in range(TT):
                        last = dve.bn_aggr(meanvar[:, t, :], stats[:, t, :])
                    last.then_inc(meanvar_ready, 1)
                elif step == "ln_norm":
                    dve.wait_ge(std_ready, n + 1)
                    dve.reciprocal(rstd[:, :], std[:, :]).then_inc(rstd_ready, 1)
                    dve.wait_ge(rstd_ready, n + 1)
                    for t in range(TT):
                        last = dve.tensor_scalar(normed[:, t, :], ps_aux[t // 2][:, (t % 2) * E:(t % 2 + 1) * E],
                                                 meanvar[:, t, 0:1], rstd[:, t:t + 1], ALU.subtract, ALU.mult)
                        if t % 2 == 1:
                            last.then_inc(aux_free[t // 2], 1)
                    dve.wait_ge(aux_free[1], p.aux[1]["out"] + 1)
                    dve.nop().then_inc(normed_ready, 1)
                elif step == "x2":
                    for c in range(CT):
                        dve.wait_ge(aux_free[c], p.aux[c]["turn"] + 1)
                        dve.tensor_tensor(x2[:, p.n_parity, c, :], x2[:, p.n_parity, c, :], xt[:, c, :], ALU.add)\
                            .then_inc(x2_ready, 1)
                elif step == "x2_lo":
                    dve.wait_ge(x2_hi_ready, n + 1)
                    lo(both(x2_lo[:, p.n_parity, :, :]), both(x2[:, p.n_parity, :, :]),
                       both(x2_hi[:, p.n_parity, :, :])).then_inc(x2_split, 1)
                elif step == "gate_part":
                    dve.wait_ge(experts_ready, f * 2 + 2)
                    for i, q in ((6, 0), (7, 1)):
                        dve.wait_ge(gate_part, f * 8 + i)
                        dve.scalar_tensor_tensor(gpart[:, :], gw1[:, q, :], y[:, 0, q, 0:1], gpart[:, :], ALU.mult,
                                                 ALU.add).then_inc(gate_part, 1)
                elif step == "gate_spread":
                    dve.wait_ge(aux_ready[0], p.aux[0]["gate_hidden"] + 1)
                    for c in range(CT):
                        last = dve.tensor_scalar(gspread[:, c, :], ones[:, :], ps_aux[0][:, c:c + 1], 0.0, ALU.mult, ALU.max)
                        last.then_inc(gate_spread, 1)
                    dve.wait_ge(gate_spread, f * 2 + 2)
                    dve.nop().then_inc(aux_free[0], 1)
                elif step == "gate_max":
                    dve.wait_ge(aux_ready[0], p.aux[0]["gate_logits"] + 1)
                    dve.tensor_reduce(gmax[:, :], ps_aux[0][:, 0:4], AX_X, ALU.max, negate=True).then_inc(gate_max, 1)
                elif step == "gate_soft":
                    dve.wait_ge(aux_free[0], p.aux[0]["gate_logits"] + 1)
                    dve.tensor_scalar(gexp[:, :], gsig[:, :], -1.0, 1.0, ALU.mult, ALU.add).then_inc(gate_soft, 1)
                    dve.wait_ge(gate_soft, f * 6 + 1)
                    dve.reciprocal(gexp[:, :], gexp[:, :]).then_inc(gate_soft, 1)
                    dve.wait_ge(gate_soft, f * 6 + 2)
                    dve.tensor_tensor(gexp[:, :], gexp[:, :], gsig[:, :], ALU.mult).then_inc(gate_soft, 1)
                    dve.wait_ge(gate_soft, f * 6 + 3)
                    dve.tensor_reduce(gsum[:, :], gexp[:, :], AX_X, ALU.add).then_inc(gate_soft, 1)
                    dve.wait_ge(gate_soft, f * 6 + 4)
                    dve.reciprocal(grec[:, :], gsum[:, :]).then_inc(gate_soft, 1)
                    dve.wait_ge(gate_soft, f * 6 + 5)
                    dve.tensor_scalar(g[:, :], gexp[:, :], grec[:, :], None, ALU.mult).then_inc(gate_soft, 1)
                elif step in ("mix0", "mix1", "mix2", "mix3"):
                    mix(f, p.f_parity, int(step[-1]))

            done = [0]

            def step(ins):
                done[0] += 1
                ins.then_inc(consts_chain, 1)

            def sync():
                dve.wait_ge(consts_chain, done[0])

            dve.wait_ge(par_loaded, 16)
            step(dve.memset(ones[:, :], 1.0))
            step(dve.memset(eps[:, :], LN_EPS))
            step(dve.tensor_reduce(soft[:, 0:2], par[:, C_BLEND:C_BLEND + CT * D].rearrange("p (c d) -> p c d", c=CT),
                                   AX_X, ALU.max, negate=True))
            step(dve.tensor_reduce(soft[:, 10:13], par[:, C_GV:C_GV + TYPES * NE].rearrange("p (t e) -> p t e", t=TYPES),
                                   AX_X, ALU.max, negate=True))
            sync()
            step(dve.tensor_scalar(soft[:, 4:7], soft[:, 10:13], 10.0, None, ALU.mult))
            sync()
            dve.nop().then_inc(consts_ready, 1)
            dve.wait_ge(types_loaded, 32)
            step(dve.tensor_copy(types_f[:, :], types_b[:, :]))
            dve.wait_ge(alpha_exp, 1 + CT + TYPES)
            step(dve.tensor_scalar(alpha[:, :], alpha[:, :], 1.0, None, ALU.add))
            step(dve.reciprocal(soft[:, 10:15], soft[:, 2:4] if False else soft[:, 2:7]))
            sync()
            step(dve.reciprocal(alpha[:, :], alpha[:, :]))
            for c in range(CT):
                step(dve.tensor_scalar(blend_w[:, c, :], blend_w[:, c, :], soft[:, 10 + c:11 + c], None, ALU.mult))
            dve.wait_ge(wc_hi_ready, 1)
            lo(wc_lo[:, :], y[:, :, :, :].rearrange("p i c t -> p (i c t)")[:, 0:W_ALL], wc_hi[:, :])\
                .then_inc(wc_ready, 1)
            sync()
            step(dve.reciprocal(soft[:, 10:13], soft[:, 7:10]))
            sync()
            for t in range(TYPES):
                for s in range(2):
                    step(dve.tensor_scalar(pairs_s[:, 2 * t + s:2 * t + s + 1], pairs[:, t, t + s:t + s + 1],
                                           soft[:, 10 + t:11 + t], None, ALU.mult))
                step(dve.tensor_scalar(picks[:, t, :], types_f[:, :], float(t), None, ALU.is_equal))
            sync()
            for t in range(TYPES):
                for s in range(2):
                    if t == 0:
                        step(dve.tensor_scalar(wab[:, s, :], picks[:, t, :], pairs_s[:, s:s + 1], None, ALU.mult))
                    else:
                        step(dve.scalar_tensor_tensor(wab[:, s, :], picks[:, t, :], pairs_s[:, 2 * t + s:2 * t + s + 1],
                                                      wab[:, s, :], ALU.mult, ALU.add))
                sync()
            dve.wait_ge(gw1_loaded, 16)

            way = drive("vector", mixture, beside)
            next(way)
            relu_lo(0, 0)
            relu_lo(0, 1)
            next(way)
            add_expert_b(B - 1)
            for _ in way:
                pass

        @block.gpsimd
        def _(pool):
            def wi_rest(b, u):
                b, u, count, buf = unit_of(b, u)
                pool.wait_ge(wi_hi_ready, count + 1)
                pool.tensor_tensor(wi_lo[:, buf, :], raw_wi[:, buf, :], f32(wi_hi[:, buf, :]), ALU.subtract)\
                    .then_inc(wi_ready, 1)

            def wo_rest(b, u):
                b, u, count, buf = unit_of(b, u)
                pool.wait_ge(wo_hi_ready, count + 1)
                pool.tensor_tensor(wo_lo[:, buf, :], raw_wo[:, buf, :], f32(wo_hi[:, buf, :]), ALU.subtract)\
                    .then_inc(wo_ready, 1)

            def mixture(b, k, parity, last):
                m = k // 4
                if k % 4 == 0 and not (last and m + 1 >= UNITS):
                    wo_rest(b, m + 1)
                if k % 4 == 2 and not (last and m + 2 >= UNITS):
                    wi_rest(b, m + 2)

            wi_rest(0, 0)
            wo_rest(0, 0)
            wi_rest(0, 1)
            for _ in drive("gpsimd", mixture, None):
                pass


def kernel(**inputs):
    import concourse.bacc as bacc
    from concourse.bass_utils import run_bass_kernel_spmd

    a = {k: np.asarray(v) for k, v in inputs.items()}

    def rows(w):
        k, n = w.shape[0] // P, w.shape[1]
        return w.reshape(k, P, n).transpose(1, 0, 2).reshape(P, k * n)

    def cols(v):
        return v.reshape(-1, P).T

    def padded(w, r, c):
        out = np.zeros((r, c), np.float32)
        out[:w.shape[0], :w.shape[1]] = w
        return out

    def every(v):
        return np.tile(v.reshape(1, -1), (P, 1))

    w_ctx = np.concatenate([
        rows(a["L0_cond_Wg"].T), rows(a["L0_cond_Wsoma"].T), rows(a["L0_cond_Wtemp"].T), rows(a["L0_cond_Wout"].T),
        rows(padded(a["L0_cond_Wn1"].T, E, P)), padded(a["cond_256"].T, P, P)], axis=1)
    params = np.concatenate([
        cols(a["L0_cond_bg"]), cols(a["L0_cond_bsoma"]), cols(a["L0_cond_btemp"]), cols(a["L0_cond_gamma"]),
        cols(a["L0_cond_beta"]), padded(a["L0_cond_bn1"][:, None], P, 1), padded(a["condB_bn2"][:, None], P, 1),
        a["cond_1024"].reshape(D, CT, P).transpose(2, 1, 0).reshape(P, CT * D),
        every(np.concatenate([a["condB_tauraws"], a["L0_cond_tau_ctx"].reshape(1)])),
        every(a["L1_cond_gate_vecs"]), rows(a["L1_cond_gate_w2"])], axis=1)

    def wi_units(w):
        return w.reshape(-1, CT, P, 2, UF).transpose(0, 3, 2, 1, 4).reshape(-1, 2, P, CT * UF)

    def wo_units(w):
        return w.reshape(-1, 2, UT, P, E).transpose(0, 1, 3, 2, 4).reshape(-1, 2, P, UT * E)

    sent = {
        "x": np.concatenate([a["x"].reshape(B, T, CT, P).transpose(0, 3, 2, 1).reshape(B, P, CT * T),
                             np.zeros((1, P, CT * T), np.float32)]),
        "w_ctx": np.stack([w_ctx, padded(np.eye(P, dtype=np.float32), P, w_ctx.shape[1])]),
        "params": params,
        "types_row": a["itok_B_0_2"].reshape(1, B),
        "types_all": every(a["itok_B_0_2"]),
        "shared_wi": wi_units(a["L1_cond_share_wi"]),
        "shared_wo": wo_units(a["L1_cond_share_wo"]),
        "expert_wi": wi_units(a["L1_cond_expert_wi"]),
        "expert_wo": wo_units(a["L1_cond_expert_wo"]),
        "gate_w1": rows(a["L1_cond_gate_w1"]),
    }
    nc = bacc.Bacc("TRN2", target_bir_lowering=False, num_devices=1)
    arrays, args = {}, []
    for name, v in sent.items():
        v = np.ascontiguousarray(v)
        arrays[f"in_{name}"] = v
        args.append(nc.dram_tensor(f"in_{name}", v.shape, mybir.dt.from_np(v.dtype), kind="ExternalInput").ap())
    args.append(nc.dram_tensor("out_t", (B, P, CT * T), F32, kind="ExternalOutput").ap())
    build(nc, *args)
    r = run_bass_kernel_spmd(nc, [arrays], core_ids=[0])
    got = np.asarray(r.results[0]["out_t"])
    return np.ascontiguousarray(got.reshape(B, P, CT, T).transpose(0, 3, 2, 1).reshape(B, T, E))
```

```python
from contextlib import ExitStack

import numpy as np

import concourse.bass as bass
from concourse import mybir

ALU = mybir.AluOpType
ACT = mybir.ActivationFunctionType
F32 = mybir.dt.float32
F32R = mybir.dt.float32r
I32 = mybir.dt.int32
AX_X = mybir.AxisListType.X

P = 128
B, T, E = 8, 512, 256
CT = E // P
D = 8
H1 = P // 2
F = 1024
NE = 4
NS = 3
TYPES = 3
FFNS = NS + 2
UF = F // 2
UT = UF // P
UNITS = FFNS * F // UF
TPF = F // P
SLOTS = FFNS * TPF
LAG = 2
NU = 4
TT = T // P
LN_EPS = 1e-5

W_N1, W_N2, W_GATE, W_SOMA, W_TEMP, W_OUT, W_ALL = np.cumsum(
    [0, CT * P, P, 2 * CT * E, CT * E, CT * E, CT * E]).tolist()
W_PARTS = (slice(0, W_GATE), slice(W_GATE, W_SOMA), slice(W_SOMA, W_ALL))
(C_BG, C_BSOMA, C_BTEMP, C_GAMMA, C_BETA, C_BN1, C_BN2, C_BLEND, C_TAU, C_GV, C_ALL) = np.cumsum(
    [0, CT, CT, CT, CT, CT, 1, 1, CT * D, D + 1, TYPES * NE]).tolist()

PLAN_TENSOR = {
    0.5: ["mod_hidden"], 1.5: ["soma"], 2.5: ["mod", "gate_hidden"], 4.5: ["wgate"],
    24.5: ["tgate"], 27.5: ["out"], 31.5: ["turn"],
}
PLAN_SCALAR = {
    1: ["mod_hidden"], 2: ["soma"], 3: ["mod"], 4: ["gate_exp"], 5: ["wgate"],
    23.5: ["temp_hi"], 25: ["tgate"], 26: ["sg_hi"], 29: ["ln_sqrt"], 32.5: ["turn"], 34: ["x2_hi"],
    36: ["next_x_hi"], 38.5: ["next_ctx_hi"],
}
PLAN_VECTOR = {
    0.5: ["gate_part"], 1.5: ["mod_hidden_lo"], 3.5: ["gate_logits"],
    4.5: ["gate_soft", "mix1", "mix2"], 5.5: ["mix3"], 6: ["gated"], 6.5: ["mix0"],
    24: ["temp_lo"], 25.5: ["sg"], 26: ["sg_lo"], 28.5: ["ln_stats"], 29.5: ["ln_norm"], 33: ["x2"], 34.5: ["x2_lo"],
    36.5: ["next_x_lo"], 37: ["next_ctx_scan"], 39: ["next_ctx_lo"],
}
for _d in range(D):
    PLAN_VECTOR[7.5 + 2 * _d] = [f"ema_in{_d}"]
    PLAN_VECTOR[8.5 + 2 * _d] = [f"ema_out{_d}"]
PLAN_SYNC = {
    3: ["mod"], 4: ["modb0", "modb1"], 8: ["store"], 10: ["modb2"], 14: ["modb3"], 33: ["next_x"],
}
PLANS = {"sync": PLAN_SYNC, "tensor": PLAN_TENSOR, "scalar": PLAN_SCALAR, "vector": PLAN_VECTOR, "gpsimd": {}}


def from_slot(plan, first, head):
    return {**head, **{k: names for k, names in plan.items() if k >= first}}


FIRST_PLANS = {
    "sync": from_slot(PLAN_SYNC, 8, {4: ["mod"], 5: ["modb0", "modb1"]}),
    "tensor": from_slot(PLAN_TENSOR, 8, {3.5: ["mod"], 4.5: ["wgate"]}),
    "scalar": from_slot(PLAN_SCALAR, 8, {0.5: ["x_hi"], 1.5: ["ctx_hi"], 4: ["mod"], 5: ["wgate"]}),
    "vector": from_slot(PLAN_VECTOR, 7.5, {0.5: ["ctx_scan", "mod_hidden_lo", "x_lo"], 2: ["ctx_lo"],
                                           6: ["gated"]}),
    "gpsimd": {},
}
GATE_PART_SLOT = 33
MIX_ORDER = (1, 2, 3, 0)
OPEN_SPREAD = 2
OPEN_VECTOR_INPUTS = {0: 0, 1: 1, 4: 3, 6: 5}
HALF = T // 2
FINAL_OWN = P
FILLERS = {"x": 10, "out": 3, "normed1": 2, "x2": 7, "gate": 5, "mix": 20}
AUX_BANKS = {"mod_hidden": (0,), "mod": (1,), "gate_hidden": (0,)}
GATING = {"gate_hidden", "gate_logits", "gate_exp", "gate_part", "gate_soft",
          "mix0", "mix1", "mix2", "mix3", "store"}


def later(count):
    return not isinstance(count, int) or count > 0


def final(f):
    return isinstance(f, int) and f == B - 1


class Period:

    def __init__(self, n, f, n_parity, f_parity, aux_before, plans=PLANS):
        self.n, self.f, self.n_parity, self.f_parity, self.plans = n, f, n_parity, f_parity, plans
        orders = ([], [])
        for slot in sorted(plans["tensor"]):
            for name in self.steps("tensor", slot):
                for m in AUX_BANKS.get(name, (0, 1)):
                    orders[m].append(name)
        self.uses = [len(order) for order in orders]
        self.aux = [{name: aux_before[m] + i for i, name in enumerate(order)} for m, order in enumerate(orders)]

    def steps(self, engine, slot):
        for name in self.plans[engine].get(slot, ()):
            if (self.f if name in GATING else self.n) is not None:
                yield name


def build(nc, x, w_ctx, params, types_row, types_all, shared_wi, shared_wo, expert_wi, expert_wo,
          gate_w1, gate_w2, out):
    mod_scratch = nc.dram_tensor("mod_scratch", [D, T], F32, kind="Internal").ap()

    with ExitStack() as ctx:
        def sb(name, shape, dt=F32):
            return ctx.enter_context(nc.sbuf_tensor(name, shape, dt))

        def sem(name):
            return ctx.enter_context(nc.semaphore(name))

        def sems(name, n):
            return [sem(f"{name}{i}") for i in range(n)]

        raw_wi = sb("raw_wi", [P, 2, CT * UF])
        raw_wo = sb("raw_wo", [P, 2, UT * E])
        wi_hi = sb("wi_hi", [P, 2, CT * UF], F32R)
        wi_lo = sb("wi_lo", [P, 2, CT * UF], F32R)
        wo_hi = sb("wo_hi", [P, 2, UT * E], F32R)
        wo_lo = sb("wo_lo", [P, 2, UT * E], F32R)
        hid_hi = sb("hid_hi", [P, NU, T], F32R)
        hid_lo = sb("hid_lo", [P, NU, T], F32R)
        wc_hi = sb("wc_hi", [P, W_ALL], F32R)
        wc_lo = sb("wc_lo", [P, W_ALL], F32R)
        gw1 = sb("gw1", [P, 8, E])
        par = sb("par", [P, C_ALL])
        types_sb = sb("types_sb", [1, B], I32)
        types_b = sb("types_b", [P, B], I32)
        types_f = sb("types_f", [P, B])
        y = sb("y", [P, 5, CT, T])
        x2 = sb("x2", [P, 2, CT, T])
        x2_hi = sb("x2_hi", [P, 2, CT, T], F32R)
        x2_lo = sb("x2_lo", [P, 2, CT, T], F32R)
        xt = sb("xt", [P, CT, T])
        xg_hi = sb("xg_hi", [P, CT, T], F32R)
        xg_lo = sb("xg_lo", [P, CT, T], F32R)
        ct_hi = sb("ct_hi", [P, CT, T], F32R)
        ct_lo = sb("ct_lo", [P, CT, T], F32R)
        ctxt = sb("ctxt", [P, CT, T])
        temporal = sb("temporal", [P, CT, T])
        soma = sb("soma", [P, CT, T])
        gates = sb("gates", [P, CT, T])
        trace = sb("trace", [P, CT, T])
        modh = sb("modh", [P, T])
        modh_hi = sb("modh_hi", [P, T], F32R)
        modh_lo = sb("modh_lo", [P, T], F32R)
        mod = sb("mod", [D, T])
        modb = sb("modb", [P, 2, 2, T])
        normed = sb("normed", [P, TT, E])
        ident = sb("ident", [P, P])
        ones = sb("ones", [P, P])
        alpha = sb("alpha", [P, D + 1])
        blend_w = sb("blend_w", [P, CT, D])
        soft = sb("soft", [P, 16])
        pairs = sb("pairs", [P, TYPES, NE])
        pairs_s = sb("pairs_s", [P, 2 * TYPES])
        wab = sb("wab", [P, 2, B])
        picks = sb("picks", [P, TYPES, B])
        wa_now = sb("wa_now", [P, 2])
        gpart = sb("gpart", [P, E])
        gw2 = sb("gw2", [P, 4, E])
        logits = sb("logits", [P, 4])
        gmax = sb("gmax", [P, 1])
        gexp = sb("gexp", [P, 4])
        gsig = sb("gsig", [P, 4])
        gsum = sb("gsum", [P, 1])
        grec = sb("grec", [P, 1])
        g = sb("g", [P, 4])
        stats = sb("stats", [P, TT, 6])
        meanvar = sb("meanvar", [P, TT, 2])
        std = sb("std", [P, TT])
        rstd = sb("rstd", [P, TT])
        eps = sb("eps", [P, 1])
        warmth = sb("warmth", [P, 1])
        select = sb("select", [D, OPEN_SPREAD, P])

        ps_up = [ctx.enter_context(nc.psum_tensor(f"ps_up{i}", [P, T], F32)) for i in range(NU)]
        ps_down = [ctx.enter_context(nc.psum_tensor(f"ps_down{i}", [P, T], F32)) for i in range(CT)]
        ps_aux = [ctx.enter_context(nc.psum_tensor(f"ps_aux{i}", [P, T], F32)) for i in range(2)]

        par_loaded = sem("par_loaded")
        types_loaded = sem("types_loaded")
        wc_loaded = sems("wc_loaded", len(W_PARTS))
        ident_loaded = sem("ident_loaded")
        consts_ready = sem("consts_ready")
        consts_chain = sem("consts_chain")
        alpha_exp = sem("alpha_exp")
        blend_ready = sem("blend_ready")
        wc_hi_ready = sem("wc_hi_ready")
        wc_hi_last = sem("wc_hi_last")
        wc_ready = sems("wc_ready", len(W_PARTS))
        wi_loaded = sems("wi_loaded", 2)
        wo_loaded = sems("wo_loaded", 2)
        wi_hi_ready = sem("wi_hi_ready")
        wo_hi_ready = sem("wo_hi_ready")
        wi_ready = sem("wi_ready")
        wo_ready = sem("wo_ready")
        up_done = sem("up_done")
        hid_hi_ready = sem("hid_hi_ready")
        hid_ready = sem("hid_ready")
        down_done = sem("down_done")
        y_ready = sem("y_ready")
        experts_ready = sem("experts_ready")
        aux_ready = sems("aux_ready", 2)
        aux_free = sems("aux_free", 2)
        x_loaded = sem("x_loaded")
        x_hi_ready = sem("x_hi_ready")
        x_ready = sem("x_ready")
        ctx_ready = sem("ctx_ready")
        ctx_hi_ready = sem("ctx_hi_ready")
        ctx_split = sem("ctx_split")
        modh_hi_ready = sem("modh_hi_ready")
        modh_split = sem("modh_split")
        mod_ready = sem("mod_ready")
        mod_stored = sem("mod_stored")
        modb_loaded = sems("modb_loaded", 2)
        gated_ready = sem("gated_ready")
        ema_in = sem("ema_in")
        ema_trace = sem("ema_trace")
        ema_sum = sem("ema_sum")
        temp_hi_ready = sem("temp_hi_ready")
        temp_split = sem("temp_split")
        sg_ready = sem("sg_ready")
        sg_hi_ready = sem("sg_hi_ready")
        sg_split = sem("sg_split")
        stats_ready = sem("stats_ready")
        meanvar_ready = sem("meanvar_ready")
        std_ready = sem("std_ready")
        rstd_ready = sem("rstd_ready")
        normed_ready = sem("normed_ready")
        x2_ready = sem("x2_ready")
        x2_hi_ready = sem("x2_hi_ready")
        x2_split = sem("x2_split")
        gate_part = sem("gate_part")
        gate_logit = sem("gate_logit")
        gate_max = sem("gate_max")
        gate_sig = sem("gate_sig")
        gate_soft = sem("gate_soft")
        mixed = sem("mixed")
        wa_ready = sem("wa_ready")
        out_stored = sem("out_stored")
        last_stored = sems("last_stored", CT)
        gw1_loaded = sem("gw1_loaded")
        gw2_loaded = sem("gw2_loaded")
        final_diag = sem("final_diag")
        final_sum = sem("final_sum")
        final_added = sem("final_added")
        first_token = sem("first_token")
        warm = sem("warm")
        open_hidden = sem("open_hidden")
        open_modh = sem("open_modh")
        open_mod = sem("open_mod")
        open_modded = sem("open_modded")
        open_wgate = sem("open_wgate")
        open_wsig = sem("open_wsig")
        open_soma = sem("open_soma")
        open_select = sem("open_select")
        open_spread = sem("open_spread")
        open_modb = sems("open_modb", D // 2)
        open_diag = sem("open_diag")
        open_in_pool = sem("open_in_pool")
        open_in_dve = sem("open_in_dve")
        open_trace = sem("open_trace")
        open_sum = sem("open_sum")
        open_temp = sem("open_temp")
        open_temp_hi = sem("open_temp_hi")
        open_temp_split = sem("open_temp_split")
        open_tgate = sem("open_tgate")
        open_tsig = sem("open_tsig")
        open_sg = sem("open_sg")
        open_sg_hi = sem("open_sg_hi")
        open_sg_split = sem("open_sg_split")
        open_x1 = sem("open_x1")
        open_x1_hi = sem("open_x1_hi")
        open_soma1 = sem("open_soma1")
        open_x1_split = sem("open_x1_split")
        open_x1_done = sem("open_x1_done")
        open_out = sem("open_out")
        open_stats = sem("open_stats")
        open_meanvar = sem("open_meanvar")
        open_std = sem("open_std")
        open_rstd = sem("open_rstd")
        open_normed = sem("open_normed")
        open_turn = sem("open_turn")
        open_base = sem("open_base")
        open_x2_hi = sem("open_x2_hi")
        open_x2_split = sem("open_x2_split")

        def f32(ap):
            return ap.bitcast(F32)

        def y_at(i, parity):
            return 4 if i == 1 and parity else i

        raw_wc = y[:, :, :, :].rearrange("p i c t -> p (i c t)")
        open_modulation = y[:, 1:5, :, :]
        diag = gw1[:, :, :].rearrange("p k e -> p (k e)")
        open_traces = [trace[:, :, :], temporal[:, :, :], x2[:, 0, :, :], x2[:, 1, :, :], ctxt[:, :, :],
                       y[:, 0, :, :]]

        final_gates = normed[:, :, :].rearrange("p t e -> p (t e)")

        def half(h):
            return slice(h * HALF, (h + 1) * HALF)

        def col(c, i=0):
            return par[:, c + i:c + i + 1]

        def drive(eng, mixture, beside):
            def alone(p, slots):
                for k in slots:
                    for s in [*p.steps(eng, k), *p.steps(eng, k + 0.5)]:
                        beside(s, k, p)

            def run(b, parity, p, last):
                for k in range(SLOTS):
                    for s in p.steps(eng, k):
                        beside(s, k, p)
                    mixture(b, k, parity, last)
                    for s in p.steps(eng, k + 0.5):
                        beside(s, k, p)

            first = Period(1, None, 1, None, (0, 0), FIRST_PLANS)
            run(0, 0, first, False)
            uses = Period(2, 0, 0, 0, (0, 0)).uses
            with ENGINES[eng].Fori(0, (B - 2) // 2) as i:
                for j in range(2):
                    b = i * 2 + (1 + j)
                    p = Period(i * 2 + (2 + j), i * 2 + j, j % 2, j % 2,
                               [i * (2 * uses[m]) + (first.uses[m] + j * uses[m]) for m in range(2)])
                    run(b, (1 + j) % 2, p, False)
            last = Period(None, B - 2, None, 0, [first.uses[m] + (B - 2) * uses[m] for m in range(2)])
            run(B - 1, 1, last, True)
            yield "mixture ends"
            after = [first.uses[m] + (B - 2) * uses[m] + last.uses[m] for m in range(2)]
            alone(Period(None, B - 1, None, 1, after), range(SLOTS))

        block = ctx.enter_context(nc.Block())
        ENGINES = {"sync": nc.sync, "tensor": nc.tensor, "scalar": nc.scalar, "vector": nc.vector,
                   "gpsimd": nc.gpsimd}

        def unit_of(b, u):
            if u >= UNITS:
                b, u = b + 1, u - UNITS
            return b, u, b * UNITS + u, u % 2

        @block.sync
        def _(sp):
            expert = {}

            def load_wi(b, u):
                b, u, count, buf = unit_of(b, u)
                if later(count - 1):
                    sp.wait_ge(wi_ready, count - 1)
                sp.dma_start(raw_wi[:, buf, :], source(shared_wi, expert_wi, b, u)).then_inc(wi_loaded[buf], 16)

            def load_wo(b, u):
                b, u, count, buf = unit_of(b, u)
                if later(count - 1):
                    sp.wait_ge(wo_ready, count - 1)
                sp.dma_start(raw_wo[:, buf, :], source(shared_wo, expert_wo, b, u)).then_inc(wo_loaded[buf], 16)

            def source(shared, experts, b, u):
                ffn, half = u // 2, u % 2
                if ffn < NS:
                    return shared[ffn, half]
                if (ffn, half) == (NS, 0) and shared is shared_wi:
                    at = b if isinstance(b, int) else bass.ds(b, 1)
                    cell = types_sb[0:1, b:b + 1] if isinstance(b, int) else types_sb[0:1, at]
                    expert["now"] = sp.value_load(cell, min_val=0, max_val=TYPES - 1)
                e = expert["now"] + (ffn - NS)
                return experts[bass.ds(e, 1), half].rearrange("o p f -> (o p) f")

            def load_x(m):
                if later(m * 2):
                    sp.wait_ge(x2_ready, m * 2)
                row = x[m] if isinstance(m, int) else x[bass.ds(m, 1)].rearrange("o p f -> (o p) f")
                sp.dma_start(xt[:, :, :].rearrange("p c t -> p (c t)"), row).then_inc(x_loaded, 16)

            def mixture(b, k, parity, last):
                m = k // 4
                if k % 4 == 0 and not (last and m + 3 >= UNITS):
                    load_wi(b, m + 3)
                if k % 4 == 1 and not (last and m + 3 >= UNITS):
                    load_wo(b, m + 3)

            def beside(step, k, p):
                n, f = p.n, p.f
                if step == "next_x":
                    load_x(n + 1)
                elif step == "mod":
                    sp.wait_ge(mod_ready, n + 1)
                    sp.dma_start(mod_scratch, mod[:, :]).then_inc(mod_stored, 16)
                elif step.startswith("modb"):
                    q = int(step[-1])
                    if q == 0:
                        sp.wait_ge(mod_stored, n * 16 + 16)
                    if q >= 2:
                        sp.wait_ge(ema_in, (n - 1) * (2 * D) + 4 * (q - 1))
                    sp.dma_start(modb[:, q % 2, :, :], mod_scratch[2 * q:2 * q + 2, :].partition_broadcast(P))\
                        .then_inc(modb_loaded[q % 2], 16)
                elif step == "store" and final(f):
                    for c in range(CT):
                        sp.wait_ge(mixed, f * 8 + 7 + c)
                        if c == 1:
                            sp.wait_ge(final_added, 1)
                        sp.dma_start(out[f][:, c * T:(c + 1) * T], x2[:, p.f_parity, c, :]).then_inc(last_stored[c], 16)
                elif step == "store":
                    sp.wait_ge(mixed, f * 8 + 8)
                    row = out[f] if isinstance(f, int) else out[bass.ds(f, 1)].rearrange("o p f -> (o p) f")
                    sp.dma_start(row, x2[:, p.f_parity, :, :].rearrange("p c t -> p (c t)")).then_inc(out_stored, 16)

            sp.dma_start(par[:, :], params).then_inc(par_loaded, 16)
            load_x(0)
            for i, part in enumerate(W_PARTS):
                sp.dma_start(raw_wc[:, part], w_ctx[0][:, part]).then_inc(wc_loaded[i], 16)
            sp.dma_start(ident[:, :], w_ctx[1][:, 0:P]).then_inc(ident_loaded, 16)
            sp.dma_start(types_sb[:, :], types_row).then_inc(types_loaded, 16)
            sp.dma_start(types_b[:, :], types_all).then_inc(types_loaded, 16)
            load_wi(0, 0)
            load_wo(0, 0)
            load_wi(0, 1)
            sp.wait_ge(mod_ready, 1)
            sp.dma_start(mod_scratch, mod[:, :]).then_inc(mod_stored, 16)
            sp.wait_ge(mod_stored, 16)
            for i in range(len(W_PARTS)):
                sp.wait_ge(wc_ready[i], 1)
            for q in range(OPEN_SPREAD // 2, D // 2):
                sp.dma_start(open_modulation[:, q, :, :], mod_scratch[2 * q:2 * q + 2, :].partition_broadcast(P))\
                    .then_inc(open_modb[q], 16)
            load_wo(0, 1)
            sp.dma_start(y[:, 1, :, :].rearrange("p c t -> p (c t)"), x[1]).then_inc(open_x1, 16)
            sp.wait_ge(open_sum, (D - 1) * CT)
            sp.dma_start(gw1[:, :, :].rearrange("p k e -> p (k e)"), gate_w1).then_inc(gw1_loaded, 16)
            sp.dma_start(gw2[:, :, :].rearrange("p k e -> p (k e)"), gate_w2).then_inc(gw2_loaded, 16)
            sp.wait_ge(types_loaded, 32)
            load_wi(0, 2)
            load_wo(0, 2)
            load_x(1)
            for _ in drive("sync", mixture, beside):
                pass
            sp.wait_ge(out_stored, (B - 1) * 16)
            for c in range(CT):
                sp.wait_ge(last_stored[c], 16)

        @block.tensor
        def _(pe):
            def product(ps, w_hi, w_lo, x_hi, x_lo, start, stop):
                pe.matmul(ps, w_hi, x_hi, start=start, stop=False)
                pe.matmul(ps, w_hi, x_lo, start=False, stop=False)
                return pe.matmul(ps, w_lo, x_hi, start=False, stop=stop)

            def up(b, k, parity, tokens=slice(0, T), done=True):
                u, j = k // UT, k % UT
                if k == 0 and tokens.stop == T:
                    pe.wait_ge(x2_split, b + 1)
                if j == 0:
                    pe.wait_ge(wi_ready, b * UNITS + (u + 1))
                ps = ps_up[k % NU][:, tokens]
                for c in range(CT):
                    at = slice(c * UF + j * P, c * UF + (j + 1) * P)
                    mm = product(ps, wi_hi[:, u % 2, at], wi_lo[:, u % 2, at], x2_hi[:, parity, c, tokens],
                                 x2_lo[:, parity, c, tokens], c == 0, c == CT - 1)
                if done:
                    mm.then_inc(up_done, 1)

            def down(b, k):
                u, j = k // UT, k % UT
                ffn = k // TPF
                if j == 0:
                    pe.wait_ge(wo_ready, b * UNITS + (u + 1))
                pe.wait_ge(hid_ready, b * SLOTS + (k + 1))
                for c in range(CT):
                    at = slice(j * E + c * P, j * E + (c + 1) * P)
                    if k % TPF == 0 and ffn == 0 and later(b * 2):
                        pe.wait_ge(experts_ready, b * 2 - (1 - c))
                    if k % TPF == 0 and ffn > 0:
                        pe.wait_ge(y_ready, b * 8 + (2 * ffn - 1 + c))
                    mm = product(ps_down[c][:, :], wo_hi[:, u % 2, at], wo_lo[:, u % 2, at], hid_hi[:, k % NU, :],
                                 hid_lo[:, k % NU, :], k % TPF == 0, k % TPF == TPF - 1)
                mm.then_inc(down_done, 1)

            def mixture(b, k, parity, last):
                if isinstance(b, int) and b == 0 and k == 0:
                    pe.wait_ge(open_modh, 2)
                    pe.wait_ge(open_soma1, CT)
                if k + LAG < SLOTS:
                    up(b, k + LAG, parity)
                elif not last:
                    up(b + 1, k + LAG - SLOTS, 1 - parity)
                down(b, k)

            def modulation(ps):
                at = slice(W_N2, W_N2 + P)
                pe.matmul(ps, wc_hi[:, at], modh_hi[:, :], start=True, stop=False)
                return pe.matmul(ps, wc_hi[0:H1, at], modh_lo[0:H1, :], start=False, stop=True)

            def project(p, stage, terms):
                for m in range(CT):
                    if later(p.aux[m][stage]):
                        pe.wait_ge(aux_free[m], p.aux[m][stage])
                    for i, (w, xh, xl) in enumerate(terms):
                        at = slice(w + m * P, w + (m + 1) * P)
                        mm = product(ps_aux[m][:, :], wc_hi[:, at], wc_lo[:, at], xh, xl, i == 0, i == len(terms) - 1)
                    mm.then_inc(aux_ready[m], 1)

            def beside(step, k, p):
                n, f = p.n, p.f
                x_terms = lambda w: [(w + c * E, xg_hi[:, c, :], xg_lo[:, c, :]) for c in range(CT)]
                c_terms = lambda w: [(w + c * E, ct_hi[:, c, :], ct_lo[:, c, :]) for c in range(CT)]
                if step == "soma":
                    project(p, "soma", x_terms(W_SOMA))
                elif step == "mod_hidden":
                    pe.wait_ge(x_ready, n + 1)
                    if later(p.aux[0]["mod_hidden"]):
                        pe.wait_ge(aux_free[0], p.aux[0]["mod_hidden"])
                    for c in range(CT):
                        at = slice(W_N1 + c * P, W_N1 + (c + 1) * P)
                        mm = product(ps_aux[0][:, :], wc_hi[:, at], wc_lo[:, at], xg_hi[:, c, :], xg_lo[:, c, :],
                                     c == 0, c == CT - 1)
                    mm.then_inc(aux_ready[0], 1)
                elif step == "mod":
                    pe.wait_ge(modh_split, n + 1)
                    if later(p.aux[1]["mod"]):
                        pe.wait_ge(aux_free[1], p.aux[1]["mod"])
                    modulation(ps_aux[1][:, :]).then_inc(aux_ready[1], 1)
                elif step == "wgate":
                    pe.wait_ge(ctx_split, n + 1)
                    project(p, "wgate", x_terms(W_GATE) + c_terms(W_GATE + CT * E))
                elif step == "tgate":
                    pe.wait_ge(temp_split, n)
                    project(p, "tgate", c_terms(W_TEMP))
                elif step == "out":
                    pe.wait_ge(sg_split, n)
                    for t in range(TT):
                        bank = t // 2
                        if t % 2 == 0:
                            if later(p.aux[bank]["out"]):
                                pe.wait_ge(aux_free[bank], p.aux[bank]["out"])
                        for c in range(CT):
                            tok = slice(t * P, (t + 1) * P)
                            at = slice(W_OUT + c * E, W_OUT + (c + 1) * E)
                            mm = product(ps_aux[bank][:, (t % 2) * E:(t % 2 + 1) * E], xg_hi[:, c, tok],
                                         xg_lo[:, c, tok], wc_hi[:, at], wc_lo[:, at], c == 0, c == CT - 1)
                        if t % 2 == 1:
                            mm.then_inc(aux_ready[bank], 1)
                elif step == "turn":
                    pe.wait_ge(normed_ready, n)
                    for c in range(CT):
                        if later(p.aux[c]["turn"]):
                            pe.wait_ge(aux_free[c], p.aux[c]["turn"])
                        for t in range(TT):
                            mm = pe.transpose(ps_aux[c][:, t * P:(t + 1) * P], normed[:, t, c * P:(c + 1) * P], ident[:, :])
                        mm.then_inc(aux_ready[c], 1)
                elif step == "gate_hidden":
                    pe.wait_ge(gate_part, f * 8 + 8)
                    if later(p.aux[0]["gate_hidden"]):
                        pe.wait_ge(aux_free[0], p.aux[0]["gate_hidden"])
                    pe.matmul(ps_aux[0][:, 0:E], ones[:, :], gpart[:, :], start=True, stop=True).then_inc(aux_ready[0], 1)

            def context(ps, w, xh, xl, start, stop, m=0):
                at = slice(w + m * P, w + (m + 1) * P)
                return product(ps, wc_hi[:, at], wc_lo[:, at], xh, xl, start, stop)

            def fill(place, bank=ps_down[0]):
                for _ in range(FILLERS[place]):
                    pe.matmul(bank[:, 0:P], ones[:, :], ones[:, :], start=True, stop=True)

            def next_x_terms(bank, w, m, width):
                pe.wait_ge(open_x1_split, 1)
                pe.wait_ge(open_tsig, 2 + 2 * m)
                for c in range(CT):
                    mm = context(bank[:, :], w + c * width, x2_hi[:, 1, c, :], x2_lo[:, 1, c, :], c == 0, c == CT - 1, m)
                return mm

            def opening():
                pe.wait_ge(consts_ready, 1)
                fill("x")
                pe.wait_ge(wc_ready[0], 1)
                pe.wait_ge(x_ready, 1)
                for c in range(CT):
                    mm = context(ps_up[0][:, :], W_N1 + c * P, xg_hi[:, c, :], xg_lo[:, c, :], c == 0, c == CT - 1)
                mm.then_inc(open_hidden, 1)
                pe.wait_ge(wc_ready[1], 1)
                for m in range(CT):
                    for c in range(CT):
                        context(ps_aux[m][:, :], W_GATE + c * E, xg_hi[:, c, :], xg_lo[:, c, :], c == 0, False, m)
                pe.wait_ge(modh_split, 1)
                modulation(ps_up[1][:, :]).then_inc(open_mod, 1)
                pe.wait_ge(ctx_split, 1)
                for m in range(CT):
                    for c in range(CT):
                        mm = context(ps_aux[m][:, :], W_GATE + (CT + c) * E, ct_hi[:, c, :], ct_lo[:, c, :], False,
                                     c == CT - 1, m)
                    mm.then_inc(open_wgate, 1)
                pe.wait_ge(open_select, OPEN_SPREAD)
                pe.wait_ge(mod_ready, 1)
                for d in range(OPEN_SPREAD):
                    pe.matmul(ps_up[d][:, :], select[:, d, :], mod[:, :], start=True, stop=True).then_inc(open_spread, 1)
                pe.wait_ge(wc_ready[2], 1)
                for m in range(CT):
                    for c in range(CT):
                        mm = context(ps_up[2 + m][:, :], W_SOMA + c * E, xg_hi[:, c, :], xg_lo[:, c, :], c == 0,
                                     c == CT - 1, m)
                    mm.then_inc(open_soma, 1)
                for d in range(D - 1):
                    for c in range(CT):
                        at = d * CT + c
                        pe.wait_ge(open_diag, at + 1)
                        pe.wait_ge(open_trace, at + 1)
                        pe.matmul(ps_down[c][:, :], diag[:, at * P:(at + 1) * P],
                                  open_traces[d % len(open_traces)][:, c, :], start=(d == 0), stop=(d == D - 2))\
                            .then_inc(open_sum, 1)
                for m in range(CT):
                    for c in range(CT):
                        pe.wait_ge(open_temp_split, c + 1)
                        mm = context(ps_aux[m][:, :], W_TEMP + c * E, ct_hi[:, c, :], ct_lo[:, c, :], c == 0,
                                     c == CT - 1, m)
                    mm.then_inc(open_tgate, 1)
                next_x_terms(ps_aux[0], W_SOMA, 0, E).then_inc(open_x1_done, 1)
                fill("out")
                for h in range(2):
                    pe.wait_ge(open_sg_split, 3 + h)
                    for t in range(2):
                        for c in range(CT):
                            tok = slice((2 * h + t) * P, (2 * h + t + 1) * P)
                            at = slice(W_OUT + c * E, W_OUT + (c + 1) * E)
                            mm = product(ps_up[h][:, t * E:(t + 1) * E], xg_hi[:, c, tok], xg_lo[:, c, tok],
                                         wc_hi[:, at], wc_lo[:, at], c == 0, c == CT - 1)
                    mm.then_inc(open_out, 1)
                pe.wait_ge(ident_loaded, 16)
                for h in range(2):
                    if h == 0:
                        next_x_terms(ps_aux[1], W_SOMA, 1, E).then_inc(open_x1_done, 1)
                    else:
                        next_x_terms(ps_down[1], W_N1, 0, P).then_inc(open_x1_done, 1)
                        fill("normed1")
                    pe.wait_ge(open_normed, h + 1)
                    for c in range(CT):
                        for t in range(2):
                            mm = pe.transpose(ps_up[2 + h][:, c * HALF + t * P:c * HALF + (t + 1) * P],
                                              normed[:, 2 * h + t, c * P:(c + 1) * P], ident[:, :])
                    mm.then_inc(open_turn, 1)
                fill("x2")

            opening()
            pe.wait_ge(open_x2_split, 1)
            for h in range(2):
                for k in range(LAG):
                    up(0, k, 0, half(h), done=(h == 1))
            way = drive("tensor", mixture, beside)
            next(way)
            fill("gate", ps_aux[1])
            for _ in way:
                pass
            fill("mix", ps_aux[1])
            pe.wait_ge(experts_ready, B * 2)
            for at, i in enumerate(MIX_ORDER):
                pe.wait_ge(final_diag, at + 1)
                mm = pe.matmul(ps_aux[1][:, FINAL_OWN:T], final_gates[:, i * P:(i + 1) * P],
                               y[:, y_at(i, (B - 1) % 2), 1, FINAL_OWN:T], start=(at == 0), stop=(at == 3))
            mm.then_inc(final_sum, 1)

        @block.scalar
        def _(act):
            def hi(out_ap, in_ap):
                return act.activation(out_ap, in_ap, ACT.Copy)

            def both(t):
                return t[:, :, :].rearrange("p c t -> p (c t)")

            def wi_round(b, u):
                b, u, count, buf = unit_of(b, u)
                act.wait_ge(wi_loaded[buf], b * (UNITS // 2 * 16) + 16 * (u // 2 + 1))
                if later(count * UT - UT):
                    act.wait_ge(up_done, count * UT - UT)
                hi(wi_hi[:, buf, :], raw_wi[:, buf, :]).then_inc(wi_hi_ready, 1)

            def wo_round(b, u):
                b, u, count, buf = unit_of(b, u)
                act.wait_ge(wo_loaded[buf], b * (UNITS // 2 * 16) + 16 * (u // 2 + 1))
                if later(count * UT - UT):
                    act.wait_ge(down_done, count * UT - UT)
                hi(wo_hi[:, buf, :], raw_wo[:, buf, :]).then_inc(wo_hi_ready, 1)

            def relu(b, k):
                act.wait_ge(up_done, b * SLOTS + (k + 1))
                if later(b * SLOTS + (k + 1 - NU)):
                    act.wait_ge(down_done, b * SLOTS + (k + 1 - NU))
                act.activation(hid_hi[:, k % NU, :], ps_up[k % NU][:, :], ACT.Relu).then_inc(hid_hi_ready, 1)

            def read_out(b, ffn, parity):
                act.wait_ge(down_done, b * SLOTS + (ffn + 1) * TPF)
                if later(b * 8):
                    act.wait_ge(mixed, (b - 1) * 8 + (2 * ffn + 2 if ffn else 0))
                if ffn == NS:
                    act.wait_ge(wa_ready, b + 1)
                for c in range(CT):
                    scale = wa_now[:, 0:1] if ffn == NS else 1.0
                    act.activation(y[:, y_at((ffn + 1) % (NS + 1), parity), c, :], ps_down[c][:, :], ACT.Copy, scale=scale)\
                        .then_inc(y_ready, 1)

            def mixture(b, k, parity, last):
                if k % TPF == 0 and k > 0:
                    read_out(b, k // TPF - 1, parity)
                if k + LAG < SLOTS:
                    relu(b, k + LAG)
                elif not last:
                    relu(b + 1, k + LAG - SLOTS)
                m = k // 4
                if k % 4 == 0 and not (last and m + 1 >= UNITS):
                    wo_round(b, m + 1)
                if k % 4 == 2 and not (last and m + 2 >= UNITS):
                    wi_round(b, m + 2)

            def beside(step, k, p):
                n, f = p.n, p.f
                if step in ("x_hi", "next_x_hi"):
                    m = n + (step == "next_x_hi")
                    act.wait_ge(x_loaded, m * 16 + 16)
                    hi(both(xg_hi), both(xt)).then_inc(x_hi_ready, 1)
                elif step in ("ctx_hi", "next_ctx_hi"):
                    m = n + (step == "next_ctx_hi")
                    act.wait_ge(ctx_ready, m * 2 + 2)
                    hi(both(ct_hi), both(ctxt)).then_inc(ctx_hi_ready, 1)
                elif step == "soma":
                    for c in range(CT):
                        act.wait_ge(aux_ready[c], p.aux[c]["soma"] + 1)
                        act.activation(soma[:, c, :], ps_aux[c][:, :], ACT.Gelu, bias=col(C_BSOMA, c))\
                            .then_inc(aux_free[c], 1)
                elif step == "mod_hidden":
                    act.wait_ge(aux_ready[0], p.aux[0]["mod_hidden"] + 1)
                    act.activation(modh[:, :], ps_aux[0][:, :], ACT.Gelu, bias=col(C_BN1)).then_inc(aux_free[0], 1)
                    act.wait_ge(aux_free[0], p.aux[0]["mod_hidden"] + 1)
                    hi(modh_hi[:, :], modh[:, :]).then_inc(modh_hi_ready, 1)
                elif step == "mod":
                    act.wait_ge(aux_ready[1], p.aux[1]["mod"] + 1)
                    act.activation(mod[:, :], ps_aux[1][0:D, :], ACT.Sigmoid, bias=par[0:D, C_BN2:C_BN2 + 1])\
                        .then_inc(aux_free[1], 1)
                    act.wait_ge(aux_free[1], p.aux[1]["mod"] + 1)
                    act.nop().then_inc(mod_ready, 1)
                elif step in ("wgate", "tgate"):
                    bias = {"wgate": C_BG, "tgate": C_BTEMP}[step]
                    for c in range(CT):
                        act.wait_ge(aux_ready[c], p.aux[c][step] + 1)
                        act.activation(gates[:, c, :], ps_aux[c][:, :], ACT.Sigmoid, bias=col(bias, c))\
                            .then_inc(aux_free[c], 1)
                elif step == "temp_hi":
                    act.wait_ge(ema_sum, (n - 1) * (2 * D) + 2 * D)
                    hi(both(ct_hi), both(temporal)).then_inc(temp_hi_ready, 1)
                elif step == "sg_hi":
                    act.wait_ge(sg_ready, (n - 1) * 2 + 2)
                    hi(both(xg_hi), both(gates)).then_inc(sg_hi_ready, 1)
                elif step == "ln_sqrt":
                    act.wait_ge(meanvar_ready, n)
                    act.activation(std[:, :], meanvar[:, :, 1], ACT.Sqrt, bias=eps[:, :]).then_inc(std_ready, 1)
                elif step == "turn":
                    if later((n - 1) * 16):
                        act.wait_ge(out_stored, (n - 1) * 16)
                    for c in range(CT):
                        act.wait_ge(aux_ready[c], p.aux[c]["turn"] + 1)
                        act.activation(x2[:, p.n_parity, c, :], ps_aux[c][:, :], ACT.Identity, bias=col(C_BETA, c),
                                       scale=col(C_GAMMA, c)).then_inc(aux_free[c], 1)
                elif step == "x2_hi":
                    act.wait_ge(x2_ready, n * 2 + 2)
                    hi(both(x2_hi[:, p.n_parity, :, :]), both(x2[:, p.n_parity, :, :])).then_inc(x2_hi_ready, 1)
                elif step == "gate_exp":
                    act.wait_ge(gate_max, f + 1)
                    act.activation(gsig[:, :], logits[:, :], ACT.Sigmoid, bias=gmax[:, :]).then_inc(gate_sig, 1)

            def fetch_table(function):
                act.activation(warmth[:, :], eps[:, :], function).then_inc(warm, 1)

            def opening():
                act.wait_ge(par_loaded, 16)
                act.activation(alpha[:, :], par[:, C_TAU:C_TAU + D + 1], ACT.Exp).then_inc(alpha_exp, 1)
                act.wait_ge(consts_ready, 1)
                for c in range(CT):
                    act.activation(blend_w[:, c, :], par[:, C_BLEND + c * D:C_BLEND + (c + 1) * D], ACT.Exp,
                                   bias=soft[:, c:c + 1], accum_out=soft[:, 2 + c:3 + c]).then_inc(alpha_exp, 1)
                for t in range(TYPES):
                    act.activation(pairs[:, t, :], par[:, C_GV + t * NE:C_GV + (t + 1) * NE], ACT.Exp,
                                   bias=soft[:, 4 + t:5 + t], scale=10.0, accum_out=soft[:, 7 + t:8 + t])\
                        .then_inc(alpha_exp, 1)
                act.wait_ge(x_loaded, 16)
                hi(both(xg_hi), both(xt)).then_inc(x_hi_ready, 1)
                for i in range(2):
                    act.wait_ge(wc_loaded[i], 16)
                    hi(wc_hi[:, W_PARTS[i]], raw_wc[:, W_PARTS[i]]).then_inc(wc_hi_ready, 1)
                fetch_table(ACT.Gelu)
                act.wait_ge(ctx_ready, CT)
                hi(both(ct_hi), both(ctxt)).then_inc(ctx_hi_ready, 1)
                act.wait_ge(open_hidden, 1)
                act.activation(modh[:, :], ps_up[0][:, :], ACT.Gelu, bias=col(C_BN1)).then_inc(open_modh, 1)
                act.wait_ge(open_modh, 1)
                hi(modh_hi[:, :], modh[:, :]).then_inc(modh_hi_ready, 1)
                act.wait_ge(warm, 1)
                fetch_table(ACT.Sigmoid)
                act.wait_ge(open_mod, 1)
                act.activation(mod[:, :], ps_up[1][0:D, :], ACT.Sigmoid, bias=par[0:D, C_BN2:C_BN2 + 1])\
                    .then_inc(open_modded, 1)
                act.wait_ge(open_modded, 1)
                act.activation(mod[:, :], mod[:, :], ACT.Copy, bias=0.5).then_inc(mod_ready, 1)
                for c in range(CT):
                    act.wait_ge(open_wgate, c + 1)
                    act.activation(gates[:, c, :], ps_aux[c][:, :], ACT.Sigmoid, bias=col(C_BG, c)).then_inc(open_wsig, 1)
                act.wait_ge(blend_ready, CT)
                act.wait_ge(ident_loaded, 16)
                for d in range(D - 1):
                    for c in range(CT):
                        at = d * CT + c
                        act.activation(diag[:, at * P:(at + 1) * P], ident[:, :], ACT.Copy, scale=blend_w[:, c, d:d + 1])\
                            .then_inc(open_diag, 1)
                for c in range(CT):
                    act.wait_ge(open_soma, c + 1)
                    act.activation(soma[:, c, :], ps_up[2 + c][:, :], ACT.Gelu, bias=col(C_BSOMA, c))
                act.wait_ge(warm, 2)
                fetch_table(ACT.Sigmoid)
                wi_round(0, 0)
                act.wait_ge(open_x1, 16)
                hi(both(x2_hi[:, 1, :, :]), both(y[:, 1, :, :])).then_inc(open_x1_hi, 1)
                wo_round(0, 0)
                wi_round(0, 1)
                for c in range(CT):
                    act.wait_ge(open_temp, c + 1)
                    hi(ct_hi[:, c, :], open_traces[(D - 1) % len(open_traces)][:, c, :]).then_inc(open_temp_hi, 1)
                for c in range(CT):
                    act.activation(x2[:, 0, c, :], xt[:, c, :], ACT.Identity, bias=col(C_BETA, c)).then_inc(open_base, 1)
                for c in range(CT):
                    act.wait_ge(open_tgate, c + 1)
                    for h in range(2):
                        act.activation(gates[:, c, half(h)], ps_aux[c][:, half(h)], ACT.Sigmoid, bias=col(C_BTEMP, c))\
                            .then_inc(open_tsig, 1)
                    for h in range(2):
                        act.wait_ge(open_sg, 2 * c + h + 1)
                        hi(xg_hi[:, c, half(h)], gates[:, c, half(h)]).then_inc(open_sg_hi, 1)
                act.wait_ge(warm, 3)
                fetch_table(ACT.Sqrt)

                def x2_round(h):
                    act.wait_ge(x2_ready, h + 1)
                    hi(x2_hi[:, 0, :, half(h)], x2[:, 0, :, half(h)]).then_inc(open_x2_hi, 1)

                for h in range(2):
                    act.wait_ge(open_meanvar, h + 1)
                    act.activation(std[:, 2 * h:2 * h + 2], meanvar[:, 2 * h:2 * h + 2, 1], ACT.Sqrt, bias=eps[:, :])\
                        .then_inc(open_std, 1)
                act.wait_ge(warm, 4)
                fetch_table(ACT.Gelu)
                x2_round(0)
                x2_round(1)
                act.wait_ge(open_x1_done, 3)
                act.activation(modh[:, :], ps_down[1][:, :], ACT.Gelu, bias=col(C_BN1)).then_inc(open_modh, 1)
                act.wait_ge(open_modh, 2)
                hi(modh_hi[:, :], modh[:, :]).then_inc(modh_hi_ready, 1)
                for c in range(CT):
                    act.activation(soma[:, c, :], ps_aux[c][:, :], ACT.Gelu, bias=col(C_BSOMA, c)).then_inc(open_soma1, 1)

            opening()
            relu(0, 0)
            relu(0, 1)
            for _ in drive("scalar", mixture, beside):
                pass
            act.wait_ge(gate_soft, B * 6)
            for i in MIX_ORDER:
                act.activation(final_gates[:, i * P:(i + 1) * P], ident[:, :], ACT.Copy, scale=g[:, i:i + 1])\
                    .then_inc(final_diag, 1)

        @block.vector
        def _(dve):
            def lo(out_ap, in_ap, hi_ap):
                return dve.tensor_tensor(out_ap, in_ap, f32(hi_ap), ALU.subtract)

            def both(t):
                return t[:, :, :].rearrange("p c t -> p (c t)")

            def relu_lo(b, k):
                dve.wait_ge(hid_hi_ready, b * SLOTS + (k + 1))
                dve.scalar_tensor_tensor(hid_lo[:, k % NU, :], ps_up[k % NU][:, :], 0.0, f32(hid_hi[:, k % NU, :]),
                                         ALU.max, ALU.subtract).then_inc(hid_ready, 1)

            def add_expert_b(b, tokens, done, tiles=range(CT)):
                dve.wait_ge(down_done, b * SLOTS + SLOTS)
                dve.wait_ge(y_ready, b * 8 + 8)
                for c in tiles:
                    dve.scalar_tensor_tensor(y[:, 0, c, tokens], ps_down[c][:, tokens], wa_now[:, 1:2], y[:, 0, c, tokens],
                                             ALU.mult, ALU.add).then_inc(done, 1)

            def pick_weights(b):
                if later(b * 2):
                    dve.wait_ge(experts_ready, b * 2)
                source = wab[:, :, b] if isinstance(b, int) else wab[:, :, bass.ds(b, 1)].rearrange("p a o -> p (a o)")
                dve.tensor_copy(wa_now[:, :], source).then_inc(wa_ready, 1)

            def shared_gate_part(b, parity):
                dve.wait_ge(y_ready, b * 8 + 6)
                for i, q in enumerate((2, 3, 4, 5, 6, 7)):
                    first = y[:, y_at(q // 2, parity), q % 2, 0:1]
                    if i == 0:
                        last = dve.tensor_scalar(gpart[:, :], gw1[:, q, :], first, None, ALU.mult)
                    else:
                        dve.wait_ge(gate_part, b * 8 + i)
                        last = dve.scalar_tensor_tensor(gpart[:, :], gw1[:, q, :], first, gpart[:, :], ALU.mult, ALU.add)
                    last.then_inc(gate_part, 1)

            def mixture(b, k, parity, last):
                if k == 0 and not (isinstance(b, int) and b == 0):
                    add_expert_b(b - 1, slice(0, T), experts_ready)
                if k + LAG < SLOTS:
                    relu_lo(b, k + LAG)
                elif not last:
                    relu_lo(b + 1, k + LAG - SLOTS)
                if k == 0:
                    pick_weights(b)
                if k == GATE_PART_SLOT:
                    shared_gate_part(b, parity)

            def mix(f, parity, i):
                at = MIX_ORDER.index(i)
                if at == 0:
                    dve.wait_ge(gate_soft, f * 6 + 6)
                for c in range(CT):
                    if at:
                        dve.wait_ge(mixed, f * 8 + (2 * at - 1 + c))
                    dve.scalar_tensor_tensor(x2[:, parity, c, :], y[:, y_at(i, parity), c, :], g[:, i:i + 1],
                                             x2[:, parity, c, :],
                                             ALU.mult, ALU.add).then_inc(mixed, 1)

            def final_mix(parity):
                dve.wait_ge(gate_soft, (B - 1) * 6 + 6)
                dve.wait_ge(experts_ready, B * 2)
                for at, i in enumerate(MIX_ORDER):
                    for c, tokens in ((0, slice(0, T)), (1, slice(0, FINAL_OWN))):
                        if at:
                            dve.wait_ge(mixed, (B - 1) * 8 + (2 * at - 1 + c))
                        dve.scalar_tensor_tensor(x2[:, parity, c, tokens], y[:, y_at(i, parity), c, tokens], g[:, i:i + 1],
                                                 x2[:, parity, c, tokens], ALU.mult, ALU.add).then_inc(mixed, 1)
                dve.wait_ge(final_sum, 1)
                dve.tensor_tensor(x2[:, parity, 1, FINAL_OWN:T], ps_aux[1][:, FINAL_OWN:T], x2[:, parity, 1, FINAL_OWN:T],
                                  ALU.add).then_inc(final_added, 1)

            def beside(step, k, p):
                n, f = p.n, p.f
                if step in ("x_lo", "next_x_lo"):
                    m = n + (step == "next_x_lo")
                    dve.wait_ge(x_hi_ready, m + 1)
                    lo(both(xg_lo), both(xt), both(xg_hi)).then_inc(x_ready, 1)
                elif step in ("ctx_scan", "next_ctx_scan"):
                    m = n + (step == "next_ctx_scan")
                    dve.wait_ge(x_loaded, m * 16 + 16)
                    for c in range(CT):
                        dve.tensor_tensor_scan(ctxt[:, c, :], alpha[:, D:D + 1].broadcast_to([P, T]), xt[:, c, :], 0.0,
                                               ALU.mult, ALU.add).then_inc(ctx_ready, 1)
                elif step in ("ctx_lo", "next_ctx_lo"):
                    m = n + (step == "next_ctx_lo")
                    dve.wait_ge(ctx_hi_ready, m + 1)
                    lo(both(ct_lo), both(ctxt), both(ct_hi)).then_inc(ctx_split, 1)
                elif step == "mod_hidden_lo":
                    dve.wait_ge(modh_hi_ready, n + 1)
                    lo(modh_lo[:, :], modh[:, :], modh_hi[:, :]).then_inc(modh_split, 1)
                elif step == "gated":
                    for c in range(CT):
                        dve.wait_ge(aux_free[c], p.aux[c]["wgate"] + 1)
                        dve.tensor_tensor(gates[:, c, :], gates[:, c, :], xt[:, c, :], ALU.mult).then_inc(gated_ready, 1)
                elif step.startswith("ema_in"):
                    d = int(step[-1])
                    if d == 0:
                        dve.wait_ge(gated_ready, n * 2 + 2)
                    if d % 2 == 0:
                        dve.wait_ge(modb_loaded[d // 2 % 2], (n - 1) * 32 + 16 * (d // 4 + 1))
                    for c in range(CT):
                        if d:
                            dve.wait_ge(ema_sum, (n - 1) * (2 * D) + (2 * d - 1 + c))
                        dve.scalar_tensor_tensor(trace[:, c, :], modb[:, d // 2 % 2, d % 2, :], 0.5, gates[:, c, :],
                                                 ALU.add, ALU.mult).then_inc(ema_in, 1)
                    dve.wait_ge(ema_in, (n - 1) * (2 * D) + (2 * d + 1))
                    dve.tensor_tensor_scan(trace[:, 0, :], alpha[:, d:d + 1].broadcast_to([P, T]), trace[:, 0, :], 0.0,
                                           ALU.mult, ALU.add).then_inc(ema_trace, 1)
                elif step.startswith("ema_out"):
                    d = int(step[-1])
                    dve.wait_ge(ema_in, (n - 1) * (2 * D) + (2 * d + 2))
                    dve.tensor_tensor_scan(trace[:, 1, :], alpha[:, d:d + 1].broadcast_to([P, T]), trace[:, 1, :], 0.0,
                                           ALU.mult, ALU.add).then_inc(ema_trace, 1)
                    for c in range(CT):
                        dve.wait_ge(ema_trace, (n - 1) * (2 * D) + (2 * d + 1 + c))
                        if d == 0:
                            last = dve.tensor_scalar(temporal[:, c, :], trace[:, c, :], blend_w[:, c, 0:1], None, ALU.mult)
                        else:
                            last = dve.scalar_tensor_tensor(temporal[:, c, :], trace[:, c, :], blend_w[:, c, d:d + 1],
                                                            temporal[:, c, :], ALU.mult, ALU.add)
                        last.then_inc(ema_sum, 1)
                elif step == "temp_lo":
                    dve.wait_ge(temp_hi_ready, n)
                    lo(both(ct_lo), both(temporal), both(ct_hi)).then_inc(temp_split, 1)
                elif step == "sg":
                    for c in range(CT):
                        dve.wait_ge(aux_free[c], p.aux[c]["tgate"] + 1)
                        dve.tensor_tensor(gates[:, c, :], gates[:, c, :], soma[:, c, :], ALU.mult).then_inc(sg_ready, 1)
                elif step == "sg_lo":
                    dve.wait_ge(sg_hi_ready, n)
                    lo(both(xg_lo), both(gates), both(xg_hi)).then_inc(sg_split, 1)
                elif step == "ln_stats":
                    for t in range(TT):
                        dve.wait_ge(aux_ready[t // 2], p.aux[t // 2]["out"] + 1)
                        dve.bn_stats(stats[:, t, :], ps_aux[t // 2][:, (t % 2) * E:(t % 2 + 1) * E]).then_inc(stats_ready, 1)
                    dve.wait_ge(stats_ready, (n - 1) * TT + TT)
                    dve.memset(std[:, :], 0.0)
                    for t in range(TT):
                        last = dve.bn_aggr(meanvar[:, t, :], stats[:, t, :])
                    last.then_inc(meanvar_ready, 1)
                elif step == "ln_norm":
                    dve.wait_ge(std_ready, n)
                    dve.reciprocal(rstd[:, :], std[:, :]).then_inc(rstd_ready, 1)
                    dve.wait_ge(rstd_ready, n)
                    for t in range(TT):
                        last = dve.tensor_scalar(normed[:, t, :], ps_aux[t // 2][:, (t % 2) * E:(t % 2 + 1) * E],
                                                 meanvar[:, t, 0:1], rstd[:, t:t + 1], ALU.subtract, ALU.mult)
                        if t % 2 == 1:
                            last.then_inc(aux_free[t // 2], 1)
                    dve.wait_ge(aux_free[1], p.aux[1]["out"] + 1)
                    dve.nop().then_inc(normed_ready, 1)
                elif step == "x2":
                    for c in range(CT):
                        dve.wait_ge(aux_free[c], p.aux[c]["turn"] + 1)
                        dve.tensor_tensor(x2[:, p.n_parity, c, :], x2[:, p.n_parity, c, :], xt[:, c, :], ALU.add)\
                            .then_inc(x2_ready, 1)
                elif step == "x2_lo":
                    dve.wait_ge(x2_hi_ready, n)
                    lo(both(x2_lo[:, p.n_parity, :, :]), both(x2[:, p.n_parity, :, :]),
                       both(x2_hi[:, p.n_parity, :, :])).then_inc(x2_split, 1)
                elif step == "gate_part":
                    if final(f):
                        dve.wait_ge(first_token, 2)
                    else:
                        dve.wait_ge(experts_ready, f * 2 + 2)
                    for i, q in ((6, 0), (7, 1)):
                        dve.wait_ge(gate_part, f * 8 + i)
                        dve.scalar_tensor_tensor(gpart[:, :], gw1[:, q, :], y[:, 0, q, 0:1], gpart[:, :], ALU.mult,
                                                 ALU.add).then_inc(gate_part, 1)
                elif step == "gate_logits":
                    if final(f):
                        add_expert_b(f, slice(1, T), experts_ready, [0])
                    dve.wait_ge(aux_ready[0], p.aux[0]["gate_hidden"] + 1)
                    for i in range(4):
                        if i:
                            dve.wait_ge(gate_logit, f * 4 + i)
                        dve.scalar_tensor_tensor(gpart[:, :], ps_aux[0][:, 0:E], 0.0, gw2[:, i, :], ALU.max, ALU.mult,
                                                 accum_out=logits[:, i:i + 1]).then_inc(gate_logit, 1)
                    dve.wait_ge(gate_logit, f * 4 + 4)
                    dve.nop().then_inc(aux_free[0], 1)
                    dve.tensor_reduce(gmax[:, :], logits[:, :], AX_X, ALU.max, negate=True).then_inc(gate_max, 1)
                    if final(f):
                        add_expert_b(f, slice(1, T), experts_ready, [1])
                elif step == "gate_soft":
                    dve.wait_ge(gate_sig, f + 1)
                    dve.tensor_scalar(gexp[:, :], gsig[:, :], -1.0, 1.0, ALU.mult, ALU.add).then_inc(gate_soft, 1)
                    dve.wait_ge(gate_soft, f * 6 + 1)
                    dve.reciprocal(gexp[:, :], gexp[:, :]).then_inc(gate_soft, 1)
                    dve.wait_ge(gate_soft, f * 6 + 2)
                    dve.tensor_tensor(gexp[:, :], gexp[:, :], gsig[:, :], ALU.mult).then_inc(gate_soft, 1)
                    dve.wait_ge(gate_soft, f * 6 + 3)
                    dve.tensor_reduce(gsum[:, :], gexp[:, :], AX_X, ALU.add).then_inc(gate_soft, 1)
                    dve.wait_ge(gate_soft, f * 6 + 4)
                    dve.reciprocal(grec[:, :], gsum[:, :]).then_inc(gate_soft, 1)
                    dve.wait_ge(gate_soft, f * 6 + 5)
                    dve.tensor_scalar(g[:, :], gexp[:, :], grec[:, :], None, ALU.mult).then_inc(gate_soft, 1)
                elif final(f):
                    if step == "mix0":
                        final_mix(p.f_parity)
                elif step in ("mix0", "mix1", "mix2", "mix3"):
                    mix(f, p.f_parity, int(step[-1]))

            done = [0]

            def step(ins):
                done[0] += 1
                ins.then_inc(consts_chain, 1)

            def sync():
                dve.wait_ge(consts_chain, done[0])

            def maxima_and_decays():
                dve.wait_ge(par_loaded, 16)
                step(dve.memset(ones[:, :], 1.0))
                step(dve.memset(eps[:, :], LN_EPS))
                step(dve.tensor_reduce(soft[:, 0:2], par[:, C_BLEND:C_BLEND + CT * D].rearrange("p (c d) -> p c d", c=CT),
                                       AX_X, ALU.max, negate=True))
                step(dve.tensor_reduce(soft[:, 10:13], par[:, C_GV:C_GV + TYPES * NE].rearrange("p (t e) -> p t e", t=TYPES),
                                       AX_X, ALU.max, negate=True))
                sync()
                step(dve.tensor_scalar(soft[:, 4:7], soft[:, 10:13], 10.0, None, ALU.mult))
                sync()
                dve.nop().then_inc(consts_ready, 1)
                dve.wait_ge(alpha_exp, 1)
                step(dve.tensor_scalar(alpha[:, :], alpha[:, :], 1.0, None, ALU.add))
                sync()
                step(dve.reciprocal(alpha[:, :], alpha[:, :]))
                sync()

            def blend_weights():
                dve.wait_ge(alpha_exp, 1 + CT)
                step(dve.reciprocal(soft[:, 13:15], soft[:, 2:4]))
                sync()
                for c in range(CT):
                    dve.tensor_scalar(blend_w[:, c, :], blend_w[:, c, :], soft[:, 13 + c:14 + c], None, ALU.mult)\
                        .then_inc(blend_ready, 1)

            def expert_weights():
                dve.wait_ge(types_loaded, 32)
                step(dve.tensor_copy(types_f[:, :], types_b[:, :]))
                dve.wait_ge(alpha_exp, 1 + CT + TYPES)
                step(dve.reciprocal(soft[:, 10:13], soft[:, 7:10]))
                sync()
                for t in range(TYPES):
                    for s in range(2):
                        step(dve.tensor_scalar(pairs_s[:, 2 * t + s:2 * t + s + 1], pairs[:, t, t + s:t + s + 1],
                                               soft[:, 10 + t:11 + t], None, ALU.mult))
                    step(dve.tensor_scalar(picks[:, t, :], types_f[:, :], float(t), None, ALU.is_equal))
                sync()
                for t in range(TYPES):
                    for s in range(2):
                        if t == 0:
                            step(dve.tensor_scalar(wab[:, s, :], picks[:, t, :], pairs_s[:, s:s + 1], None, ALU.mult))
                        else:
                            step(dve.scalar_tensor_tensor(wab[:, s, :], picks[:, t, :], pairs_s[:, 2 * t + s:2 * t + s + 1],
                                                          wab[:, s, :], ALU.mult, ALU.add))
                    sync()

            def open_input(d):
                if d >= len(open_traces):
                    dve.wait_ge(open_sum, (d - len(open_traces) + 1) * CT)
                if d < OPEN_SPREAD:
                    dve.wait_ge(open_spread, d + 1)
                    modulation = ps_up[d][:, :]
                else:
                    dve.wait_ge(open_modb[d // 2], 16)
                    modulation = open_modulation[:, d // 2, d % 2, :]
                for c in range(CT):
                    dve.tensor_tensor(open_traces[d % len(open_traces)][:, c, :], modulation, gates[:, c, :], ALU.mult)\
                        .then_inc(open_in_dve, 1)

            def open_scan(d):
                of_pool = d not in OPEN_VECTOR_INPUTS
                before = sum((e in OPEN_VECTOR_INPUTS) != of_pool for e in range(d))
                buf = open_traces[d % len(open_traces)]
                for c in range(CT):
                    if of_pool:
                        dve.wait_ge(open_in_pool, before * CT + c + 1)
                    else:
                        dve.wait_ge(open_in_dve, before * CT + c + 1)
                    dve.tensor_tensor_scan(buf[:, c, :], alpha[:, d:d + 1].broadcast_to([P, T]), buf[:, c, :], 0.0,
                                           ALU.mult, ALU.add).then_inc(open_trace, 1)

            def open_norm_in(h):
                dve.wait_ge(open_out, h + 1)
                for t in range(2):
                    dve.bn_stats(stats[:, 2 * h + t, :], ps_up[h][:, t * E:(t + 1) * E]).then_inc(open_stats, 1)
                for t in range(2):
                    dve.wait_ge(open_stats, 2 * h + t + 1)
                    last = dve.bn_aggr(meanvar[:, 2 * h + t, :], stats[:, 2 * h + t, :])
                last.then_inc(open_meanvar, 1)

            def open_norm_out(h):
                dve.wait_ge(open_std, h + 1)
                dve.reciprocal(rstd[:, 2 * h:2 * h + 2], std[:, 2 * h:2 * h + 2]).then_inc(open_rstd, 1)
                dve.wait_ge(open_meanvar, h + 1)
                dve.wait_ge(open_rstd, h + 1)
                for t in range(2):
                    at = 2 * h + t
                    last = dve.tensor_scalar(normed[:, at, :], ps_up[h][:, t * E:(t + 1) * E], meanvar[:, at, 0:1],
                                             rstd[:, at:at + 1], ALU.subtract, ALU.mult)
                last.then_inc(open_normed, 1)

            def open_residual(h):
                dve.wait_ge(open_base, CT)
                dve.wait_ge(open_turn, h + 1)
                for c in range(CT):
                    last = dve.scalar_tensor_tensor(x2[:, 0, c, half(h)], ps_up[2 + h][:, c * HALF:(c + 1) * HALF],
                                                    col(C_GAMMA, c), x2[:, 0, c, half(h)], ALU.mult, ALU.add)
                last.then_inc(x2_ready, 1)

            def open_x2_lo(h):
                dve.wait_ge(open_x2_hi, h + 1)
                return lo(x2_lo[:, 0, :, half(h)], x2[:, 0, :, half(h)], x2_hi[:, 0, :, half(h)])

            def opening():
                maxima_and_decays()
                dve.wait_ge(x_loaded, 16)
                for c in range(CT):
                    dve.tensor_tensor_scan(ctxt[:, c, :], alpha[:, D:D + 1].broadcast_to([P, T]), xt[:, c, :], 0.0,
                                           ALU.mult, ALU.add).then_inc(ctx_ready, 1)
                dve.wait_ge(x_hi_ready, 1)
                lo(both(xg_lo), both(xt), both(xg_hi)).then_inc(x_ready, 1)
                dve.wait_ge(wc_hi_ready, 1)
                lo(wc_lo[:, 0:W_N2], raw_wc[:, 0:W_N2], wc_hi[:, 0:W_N2])
                at = slice(W_N2, W_N2 + P)
                lo(wc_hi[H1:P, at], raw_wc[H1:P, at], wc_hi[H1:P, at]).then_inc(wc_ready[0], 1)
                dve.wait_ge(wc_hi_ready, 2)
                lo(wc_lo[:, W_PARTS[1]], raw_wc[:, W_PARTS[1]], wc_hi[:, W_PARTS[1]]).then_inc(wc_ready[1], 1)
                dve.wait_ge(wc_loaded[2], 16)
                dve.tensor_copy(wc_hi[:, W_PARTS[2]], raw_wc[:, W_PARTS[2]]).then_inc(wc_hi_last, 1)
                dve.wait_ge(ctx_hi_ready, 1)
                lo(both(ct_lo), both(ctxt), both(ct_hi)).then_inc(ctx_split, 1)
                dve.wait_ge(ident_loaded, 16)
                for d in range(OPEN_SPREAD):
                    dve.tensor_scalar(select[:, d, :], ones[0:D, :], ident[0:D, d:d + 1], None, ALU.mult)\
                        .then_inc(open_select, 1)
                dve.wait_ge(modh_hi_ready, 1)
                lo(modh_lo[:, :], modh[:, :], modh_hi[:, :]).then_inc(modh_split, 1)
                blend_weights()
                expert_weights()
                for c in range(CT):
                    dve.wait_ge(open_wsig, c + 1)
                    dve.tensor_tensor(gates[:, c, :], gates[:, c, :], xt[:, c, :], ALU.mult).then_inc(gated_ready, 1)
                dve.wait_ge(gated_ready, CT)
                for d in range(D):
                    for e, place in OPEN_VECTOR_INPUTS.items():
                        if place == d:
                            open_input(e)
                    open_scan(d)
                total = open_traces[(D - 1) % len(open_traces)]
                for c in range(CT):
                    dve.wait_ge(open_trace, (D - 1) * CT + c + 1)
                    dve.wait_ge(open_sum, (D - 2) * CT + c + 1)
                    dve.wait_ge(blend_ready, CT)
                    dve.scalar_tensor_tensor(total[:, c, :], total[:, c, :], blend_w[:, c, D - 1:D], ps_down[c][:, :],
                                             ALU.mult, ALU.add).then_inc(open_temp, 1)
                for c in range(CT):
                    dve.wait_ge(open_temp_hi, c + 1)
                    lo(ct_lo[:, c, :], total[:, c, :], ct_hi[:, c, :]).then_inc(open_temp_split, 1)
                for c in range(CT):
                    for h in range(2):
                        dve.wait_ge(open_tsig, 2 * c + h + 1)
                        dve.tensor_tensor(gates[:, c, half(h)], gates[:, c, half(h)], soma[:, c, half(h)], ALU.mult)\
                            .then_inc(open_sg, 1)
                    for h in range(2):
                        dve.wait_ge(open_sg_hi, 2 * c + h + 1)
                        lo(xg_lo[:, c, half(h)], gates[:, c, half(h)], xg_hi[:, c, half(h)]).then_inc(open_sg_split, 1)
                open_norm_in(0)
                open_norm_out(0)
                open_norm_in(1)
                open_norm_out(1)
                open_residual(0)
                open_residual(1)
                open_x2_lo(0).then_inc(open_x2_split, 1)
                open_x2_lo(1).then_inc(x2_split, 1)
                dve.wait_ge(gw1_loaded, 16)
                dve.wait_ge(gw2_loaded, 16)

            opening()
            relu_lo(0, 0)
            relu_lo(0, 1)
            way = drive("vector", mixture, beside)
            next(way)
            add_expert_b(B - 1, slice(0, 1), first_token)
            for _ in way:
                pass

        @block.gpsimd
        def _(pool):
            def wi_rest(b, u):
                b, u, count, buf = unit_of(b, u)
                pool.wait_ge(wi_hi_ready, count + 1)
                pool.tensor_tensor(wi_lo[:, buf, :], raw_wi[:, buf, :], f32(wi_hi[:, buf, :]), ALU.subtract)\
                    .then_inc(wi_ready, 1)

            def wo_rest(b, u):
                b, u, count, buf = unit_of(b, u)
                pool.wait_ge(wo_hi_ready, count + 1)
                pool.tensor_tensor(wo_lo[:, buf, :], raw_wo[:, buf, :], f32(wo_hi[:, buf, :]), ALU.subtract)\
                    .then_inc(wo_ready, 1)

            def mixture(b, k, parity, last):
                m = k // 4
                if k % 4 == 0 and not (last and m + 1 >= UNITS):
                    wo_rest(b, m + 1)
                if k % 4 == 2 and not (last and m + 2 >= UNITS):
                    wi_rest(b, m + 2)

            def open_input(d):
                if d >= len(open_traces):
                    pool.wait_ge(open_sum, (d - len(open_traces) + 1) * CT)
                pool.wait_ge(open_modb[d // 2], 16)
                for c in range(CT):
                    pool.tensor_tensor(open_traces[d % len(open_traces)][:, c, :], open_modulation[:, d // 2, d % 2, :],
                                       gates[:, c, :], ALU.mult).then_inc(open_in_pool, 1)

            def opening():
                pool.wait_ge(wc_hi_last, 1)
                pool.tensor_tensor(wc_lo[:, W_PARTS[2]], raw_wc[:, W_PARTS[2]], f32(wc_hi[:, W_PARTS[2]]), ALU.subtract)\
                    .then_inc(wc_ready[2], 1)
                pool.wait_ge(gated_ready, CT)
                for d in range(D):
                    if d not in OPEN_VECTOR_INPUTS:
                        open_input(d)
                wi_rest(0, 0)
                pool.wait_ge(open_x1_hi, 1)
                pool.tensor_tensor(x2_lo[:, 1, :, :], y[:, 1, :, :], f32(x2_hi[:, 1, :, :]), ALU.subtract)\
                    .then_inc(open_x1_split, 1)
                wo_rest(0, 0)
                wi_rest(0, 1)

            opening()
            for _ in drive("gpsimd", mixture, None):
                pass


def kernel(**inputs):
    import concourse.bacc as bacc
    from concourse.bass_utils import run_bass_kernel_spmd

    a = {k: np.asarray(v) for k, v in inputs.items()}

    def rows(w):
        k, n = w.shape[0] // P, w.shape[1]
        return w.reshape(k, P, n).transpose(1, 0, 2).reshape(P, k * n)

    def cols(v):
        return v.reshape(-1, P).T

    def padded(w, r, c):
        out = np.zeros((r, c), np.float32)
        out[:w.shape[0], :w.shape[1]] = w
        return out

    def every(v):
        return np.tile(v.reshape(1, -1), (P, 1))

    w_ctx = np.concatenate([
        rows(np.tile(a["L0_cond_Wn1"].T, (1, 2))), padded(np.tile(a["cond_256"].T, (2, 1)), P, P), rows(a["L0_cond_Wg"].T),
        rows(a["L0_cond_Wsoma"].T), rows(a["L0_cond_Wtemp"].T), rows(a["L0_cond_Wout"].T)], axis=1)
    params = np.concatenate([
        cols(a["L0_cond_bg"]), cols(a["L0_cond_bsoma"]), cols(a["L0_cond_btemp"]), cols(a["L0_cond_gamma"]),
        cols(a["L0_cond_beta"]), np.tile(a["L0_cond_bn1"][:, None], (2, 1)), padded(a["condB_bn2"][:, None], P, 1),
        a["cond_1024"].reshape(D, CT, P).transpose(2, 1, 0).reshape(P, CT * D),
        every(np.concatenate([a["condB_tauraws"], a["L0_cond_tau_ctx"].reshape(1)])),
        every(a["L1_cond_gate_vecs"])], axis=1)

    def wi_units(w):
        return w.reshape(-1, CT, P, 2, UF).transpose(0, 3, 2, 1, 4).reshape(-1, 2, P, CT * UF)

    def wo_units(w):
        return w.reshape(-1, 2, UT, P, E).transpose(0, 1, 3, 2, 4).reshape(-1, 2, P, UT * E)

    sent = {
        "x": np.concatenate([a["x"].reshape(B, T, CT, P).transpose(0, 3, 2, 1).reshape(B, P, CT * T),
                             np.zeros((1, P, CT * T), np.float32)]),
        "w_ctx": np.stack([w_ctx, padded(np.eye(P, dtype=np.float32), P, w_ctx.shape[1])]),
        "params": params,
        "types_row": a["itok_B_0_2"].reshape(1, B),
        "types_all": every(a["itok_B_0_2"]),
        "shared_wi": wi_units(a["L1_cond_share_wi"]),
        "shared_wo": wo_units(a["L1_cond_share_wo"]),
        "expert_wi": wi_units(a["L1_cond_expert_wi"]),
        "expert_wo": wo_units(a["L1_cond_expert_wo"]),
        "gate_w1": rows(a["L1_cond_gate_w1"]),
        "gate_w2": every(a["L1_cond_gate_w2"].T),
    }
    nc = bacc.Bacc("TRN2", target_bir_lowering=False, num_devices=1)
    arrays, args = {}, []
    for name, v in sent.items():
        v = np.ascontiguousarray(v)
        arrays[f"in_{name}"] = v
        args.append(nc.dram_tensor(f"in_{name}", v.shape, mybir.dt.from_np(v.dtype), kind="ExternalInput").ap())
    args.append(nc.dram_tensor("out_t", (B, P, CT * T), F32, kind="ExternalOutput").ap())
    build(nc, *args)
    r = run_bass_kernel_spmd(nc, [arrays], core_ids=[0])
    got = np.asarray(r.results[0]["out_t"])
    return np.ascontiguousarray(got.reshape(B, P, CT, T).transpose(0, 3, 2, 1).reshape(B, T, E))
```
